# Optimizing a Trainium2 kernel written in Bass

```python
import numpy as np
import jax
import jax.numpy as jnp

def _softmax(x, axis=-1):
    return jax.nn.softmax(x, axis=axis)

def _gelu(x):
    return jax.nn.gelu(x, approximate=True)

def _silu(x):
    return jax.nn.silu(x)

def _sigmoid(x):
    return jax.nn.sigmoid(x)

def _layernorm(x, axis=-1, eps=1e-05):
    m = jnp.mean(x, axis=axis, keepdims=True)
    v = jnp.var(x, axis=axis, keepdims=True)
    return (x - m) / jnp.sqrt(v + eps)

def _scatter_add(tgt, idx, src, axis=0):
    return tgt.at[idx].add(src)

def _segment_sum(src, seg, n):
    return jax.ops.segment_sum(src, seg, n)
kernel_name = 'mk_xattn_ffn_d1_seqx_r4_2a7713'

def setup_inputs(seed: int=0):
    np.random.seed(seed)
    _w = jnp.asarray

    def _rec_inputs():
        import jax
        import jax.numpy as jnp
        _rk = jax.random.key(seed)
        x = -0.000125 + 0.9999 * jax.random.normal(jax.random.fold_in(_rk, 1), (2, 1024, 256), jnp.float32)
        _lenS = 1024 - jax.random.randint(jax.random.fold_in(_rk, 7), (2,), 0, max(1, 1024 // 4) + 1, jnp.int32)
        _lenS2 = 64 - jax.random.randint(jax.random.fold_in(_rk, 8), (2,), 0, max(1, 64 // 4) + 1, jnp.int32)
        _ctx_1024P = jax.random.normal(jax.random.fold_in(_rk, 11), (2, 16, 256), jnp.float32)
        _ctx_1024c = jax.random.dirichlet(jax.random.fold_in(_rk, 511), 0.3 * jnp.ones((16,), jnp.float32), (2, 64))
        _ctx_1024t = jnp.einsum('bsk,bkd->bsd', _ctx_1024c, _ctx_1024P)
        _ctx_1024t = _ctx_1024t * jax.lax.rsqrt(jnp.mean(jnp.square(_ctx_1024t)) + 1e-12) * 0.953939
        ctx_1024 = -1.52775e-05 + 0.999936 * (_ctx_1024t + 0.3 * jax.random.normal(jax.random.fold_in(_rk, 611), (2, 64, 256), jnp.float32))
        return (x, ctx_1024)
    x, ctx_1024 = _rec_inputs()

    def _L0_xattn_setup():
        import jax, jax.numpy as jnp
        import numpy as np
        B, R, U, D = (16, 512, 512, 256)
        EPS_ATT = 1e-08
        EPS_LN = 1e-06
        key = jax.random.key(seed)
        ks = jax.random.split(key, 6)
        s = 1.0 / np.sqrt(D)
        return {'Q': jax.random.normal(ks[0], (B, R, D), dtype=jnp.float32), 'K': jax.random.normal(ks[1], (B, U, D), dtype=jnp.float32), 'V': jax.random.normal(ks[2], (B, U, D), dtype=jnp.float32), 'W1': jax.random.normal(ks[3], (D, D), dtype=jnp.float32) * s, 'b1': jnp.zeros((D,), dtype=jnp.float32), 'W2': jax.random.normal(ks[4], (D, D), dtype=jnp.float32) * s, 'b2': jnp.zeros((D,), dtype=jnp.float32), 'gamma': jnp.ones((D,), dtype=jnp.float32), 'beta': jnp.zeros((D,), dtype=jnp.float32)}
    _L0_xattn_all = _L0_xattn_setup()
    _L0_xattn_in = {k: v for k, v in _L0_xattn_all.items() if k in ('W1', 'b1', 'W2', 'b2', 'gamma', 'beta')}
    del _L0_xattn_all

    def _L0_ffn_setup():
        import jax, jax.numpy as jnp
        import numpy as np
        B, T, C = (4, 512, 256)
        E, F, K = (8, 512, 2)
        key = jax.random.key(seed)
        k0, k1, k2, k3 = jax.random.split(key, 4)
        s = lambda d: 1.0 / np.sqrt(d)
        x = jax.random.normal(k0, (B, T, C), dtype=jnp.float32)
        Wr = jax.random.normal(k1, (E, C), dtype=jnp.float32) * s(C)
        W1 = jax.random.normal(k2, (E, 2 * F, C), dtype=jnp.float32) * s(C)
        W2 = jax.random.normal(k3, (E, C, F), dtype=jnp.float32) * s(F)
        return {'x': x, 'Wr': Wr, 'W1': W1, 'W2': W2}
    _L0_ffn_all = _L0_ffn_setup()
    _L0_ffn_in = {k: v for k, v in _L0_ffn_all.items() if k in ('Wr', 'W1', 'W2')}
    del _L0_ffn_all
    return {'x': x, 'ctx_1024': ctx_1024, 'L0_xattn_W1': _L0_xattn_in['W1'], 'L0_xattn_b1': _L0_xattn_in['b1'], 'L0_xattn_W2': _L0_xattn_in['W2'], 'L0_xattn_b2': _L0_xattn_in['b2'], 'L0_xattn_gamma': _L0_xattn_in['gamma'], 'L0_xattn_beta': _L0_xattn_in['beta'], 'L0_ffn_Wr': _L0_ffn_in['Wr'], 'L0_ffn_W1': _L0_ffn_in['W1'], 'L0_ffn_W2': _L0_ffn_in['W2']}

def reference(x, ctx_1024, L0_xattn_W1, L0_xattn_b1, L0_xattn_W2, L0_xattn_b2, L0_xattn_gamma, L0_xattn_beta, L0_ffn_Wr, L0_ffn_W1, L0_ffn_W2):
    import jax
    import jax.numpy as jnp

    def _L0_xattn_ref(Q, K, V, W1, b1, W2, b2, gamma, beta):
        import jax, jax.numpy as jnp
        import numpy as np
        B, R, U, D = (16, 512, 512, 256)
        EPS_ATT = 1e-08
        EPS_LN = 1e-06
        d_model = Q.shape[-1]
        scale = jnp.sqrt(jnp.asarray(d_model, jnp.float32) + EPS_ATT)
        scores = jnp.einsum('brd,bud->bru', Q, K) / scale
        att = jax.nn.softmax(scores, axis=-1)
        V_att = jnp.einsum('bru,bud->brd', att, V)

        def layer_norm(x):
            mu = jnp.mean(x, axis=-1, keepdims=True)
            var = jnp.mean(jnp.square(x - mu), axis=-1, keepdims=True)
            return gamma * (x - mu) / jnp.sqrt(var + EPS_LN) + beta
        X = layer_norm(Q + V_att)
        ffn = jnp.maximum(X @ W1 + b1, 0.0) @ W2 + b2
        return layer_norm(ffn + X)

    def _L0_ffn_ref(x, Wr, W1, W2):
        import jax, jax.numpy as jnp
        import numpy as np
        B, T, C = (4, 512, 256)
        E, F, K = (8, 512, 2)
        Bb, Tt, Cc = x.shape
        flat = x.reshape(-1, Cc)
        N = flat.shape[0]
        logits = flat @ Wr.T
        weights, ids = jax.lax.top_k(logits, K)
        weights = jax.nn.softmax(weights, axis=-1)
        rows = jnp.arange(N)[:, None]
        router_weights = jnp.zeros((N, E), dtype=flat.dtype).at[rows, ids].add(weights)
        h = jnp.einsum('nc,efc->nef', flat, W1)
        val, gate = (h[..., :F], h[..., F:])
        act = val * jax.nn.silu(gate)
        expert_outputs = jnp.einsum('nef,ecf->nec', act, W2)
        out = jnp.einsum('nec,ne->nc', expert_outputs, router_weights)
        return out.reshape(Bb, Tt, Cc)
    x = x + _L0_xattn_ref(_layernorm(x, axis=-1), ctx_1024, ctx_1024, L0_xattn_W1, L0_xattn_b1, L0_xattn_W2, L0_xattn_b2, L0_xattn_gamma, L0_xattn_beta)
    x = x + _L0_ffn_ref(_layernorm(x, axis=-1), L0_ffn_Wr, L0_ffn_W1, L0_ffn_W2)
    return x

_drawn_inputs = setup_inputs


def setup_inputs(seed=0):
    import zlib

    import numpy as np

    out = dict(_drawn_inputs(seed))
    spreads = {'L0_xattn_b1': (0.0, 0.1),
     'L0_xattn_b2': (0.0, 0.1),
     'L0_xattn_gamma': (1.0, 0.2),
     'L0_xattn_beta': (0.0, 0.1)}
    factors = {}
    for name, (base, spread) in spreads.items():
        noise = np.random.default_rng([zlib.crc32(name.encode()), seed]).standard_normal(out[name].shape)
        drawn = base * np.exp(spread * noise) if base else spread * noise
        out[name] = jnp.asarray(drawn.astype(out[name].dtype))
    for name, factor in factors.items():
        out[name] = (out[name] * factor).astype(out[name].dtype)
    return out
```

```python
import concourse.bass as bass
from concourse import mybir
from contextlib import ExitStack


def xattn_then_sparse_experts(nc, x, xT, ctx_kv, aW1, aW2, vec_cols, b2, gamma, beta, WrT, eW1, eW2, flat_dram, out):
    f32, bf16, i32 = mybir.dt.float32, mybir.dt.bfloat16, mybir.dt.int32
    ACT = mybir.ActivationFunctionType
    ALU = mybir.AluOpType
    AX = mybir.AxisListType

    P = 128
    N, D = x.shape
    B, U, _ = ctx_kv.shape
    E, _, F2 = eW1.shape
    F = F2 // 2
    KD = D // P
    KF = F // P
    T = N // P
    G = 4
    NG = T // G
    TH = T // B
    TOPK = 2
    Q32 = TOPK * T
    NS = TOPK * T + E - 1
    SCALE = 1.0 / 16.0
    EPS_IN, EPS_LN = 1e-5, 1e-6
    assert D == 256 and NS % 2 == 1

    x_v = x.rearrange("(t p) c -> p t c", p=P)
    xT_v = xT.rearrange("(k p) n -> p k n", p=P)
    out_v = out[0:N, :].rearrange("(t p) c -> p t c", p=P)
    flat_v = flat_dram.rearrange("(t p) c -> p t c", p=P)
    w1_v = eW1.rearrange("e (k p) f -> p e k f", p=P)
    w2_v = eW2.rearrange("e (k p) c -> p e k c", p=P)

    ctx = ExitStack()
    with ctx:
        def sb(name, shape, dt=f32):
            return ctx.enter_context(nc.sbuf_tensor(name, shape, dt))

        def sem(name):
            return ctx.enter_context(nc.semaphore(name))

        W1 = sb("expert_w1", [P, E, KD, F2])
        W2 = sb("expert_w2", [P, E, KF, D])
        xs = sb("xs", [P, T, D])
        qu = sb("qu", [P, T, D])
        zn = sb("zn", [P, T, D])
        nf = sb("nf", [P, T, D])
        xt_area = sb("xt_area", [P, KD * N])
        xTs = xt_area[:, :].rearrange("p (k n) -> p k n", k=KD)
        nT = xt_area[:, 0:2 * KD * G * P].rearrange("p (r k n) -> p r k n", r=2, k=KD)
        hT = xt_area[:, 2 * KD * G * P:4 * KD * G * P].rearrange("p (r k n) -> p r k n", r=2, k=KD)
        prob = sb("prob", [P, T, U])
        probT = sb("probT", [U, 2, G * P])
        kv = sb("kv", [U, B, D])
        kc = prob[0:U, :, :].rearrange("p t u -> p (t u)")[:, 0:B * D].rearrange("p (b c) -> p b c", b=B)
        kT = sb("kT", [P, B, KD, U])
        aw1 = sb("aw1", [P, KD, D])
        aw1g = sb("aw1g", [P, KD, D])
        aw2 = sb("aw2", [P, KD, D])
        wr = sb("wr", [P, KD, E])
        cols = sb("cols", [P, 3, KD])
        b1f = sb("b1f", [P, KD])
        rows = sb("rows", [1, 2, D])
        bb = sb("bb", [1, D])
        gammaB = sb("gammaB", [P, D])
        betaB = sb("betaB", [P, D])
        ident = sb("ident", [P, P])
        ones_row = sb("ones_row", [1, P])
        zero = sb("zero", [P, D])
        epsr = sb("epsr", [P, 2, G, 2])
        mhalf = sb("mhalf", [P, G])
        cscale = sb("cscale", [P, G])
        cneg = sb("cneg", [P, G])
        kst = sb("kst", [U, B, 6])
        kmv = sb("kmv", [U, B, 2])
        st = sb("st", [P, G, 6])
        mv = sb("mv", [P, 4, G, 2])
        ve = sb("ve", [P, 4, T, 2])
        rstd = sb("rstd", [P, 4, T])
        mr = sb("mr", [P, 4, T])
        nmr = sb("nmr", [P, 4, T])
        r16 = sb("r16", [P, T])
        mx = sb("mx", [P, T])
        nb = sb("nb", [P, T])
        zsum = sb("zsum", [P, T])
        rz = sb("rz", [P, T])
        wts = sb("wts", [P, TOPK, T])
        prio = sb("prio", [P, E])
        tri = sb("tri", [P, P], bf16)
        onesb = sb("onesb", [P, P], bf16)
        first0 = sb("first0", [P, E, T])
        ones8 = sb("ones8", [P, E])
        iota_s = sb("iota_s", [P, NS])
        iota_p = sb("iota_p", [P, P])
        pairv = sb("pairv", [P, Q32])
        pcol = sb("pcol", [P, 2])
        eid = sb("eid", [1, NS], i32)
        slotw = sb("slotw", [P, NS])
        gi = sb("gi", [P, NS], i32)
        si = sb("si", [P, NS], i32)
        both = sb("both", [P, T * E], bf16)

        free = {"hT": 2 * KD * G * P, "prob": 0}

        def scratch(where, *dims):
            size = 1
            for d in dims:
                size *= d
            src = xt_area if where == "hT" else prob_flat
            ap = src[:, free[where]:free[where] + size]
            free[where] += size
            names = "abc"[:len(dims)]
            if len(dims) == 1:
                return ap
            return ap.rearrange(f"p ({' '.join(names)}) -> p {' '.join(names)}", **dict(zip(names, dims)))

        prob_flat = prob[:, :, :].rearrange("p t u -> p (t u)")
        lg, lg2, pick = scratch("hT", T, E), scratch("hT", T, E), scratch("hT", T, E)
        oh = scratch("hT", TOPK, T * E).rearrange("p c (t e) -> p c t e", t=T)
        rsel = scratch("hT", TOPK, T * E).rearrange("p c (t e) -> p c t e", t=T)
        totE, incl, excl = scratch("hT", E, T), scratch("hT", E, T), scratch("hT", E, T)
        base, rank = scratch("hT", T, E), scratch("hT", T, E)
        m12, pmax = scratch("hT", TOPK, T), scratch("hT", TOPK, T)
        dm, ex, den = scratch("hT", T), scratch("hT", T), scratch("hT", T)
        pos, hif, lof = scratch("hT", Q32), scratch("hT", Q32), scratch("hT", Q32)
        posi, hii, loi = (scratch("hT", Q32).bitcast(i32) for _ in range(3))
        ntf, ends, starts = scratch("prob", E), scratch("prob", E), scratch("prob", E)
        tp, nti = scratch("prob", E).bitcast(i32), scratch("prob", E).bitcast(i32)
        ge = scratch("prob", NS, E)[0:1]
        eidf = scratch("prob", NS)[0:1]
        sk, stok, padg, pads = (scratch("prob", NS) for _ in range(4))
        assert free["hT"] <= KD * N and free["prob"] <= T * U
        ohlo = qu[:, :, :].rearrange("p t c -> p (t c)").rearrange("p (q n) -> p q n", q=Q32)
        slots = zn[:, :, :].rearrange("p t c -> p (t c)")[:, 0:Q32 * 2 * NS].rearrange(
            "p (q a s) -> p q a s", q=Q32, a=2)
        ohhi = zn[:, :, :].rearrange("p t c -> p (t c)")[:, Q32 * 2 * NS:Q32 * 3 * NS].rearrange(
            "p (q s) -> p q s", q=Q32)

        at = [0]

        def area(n):
            at[0] += n
            return xt_area[:, at[0] - n:at[0]]

        X = area(2 * D).rearrange("p (b c) -> p b c", b=2)
        XT = area(2 * D).rearrange("p (b k n) -> p b k n", b=2, k=KD)
        S = area(2 * F).rearrange("p (b f) -> p b f", b=2)
        A = area(2 * F).rearrange("p (b f) -> p b f", b=2)
        AT = area(F).rearrange("p (k n) -> p k n", k=KF)
        Y = area(2 * D).rearrange("p (b c) -> p b c", b=2)

        bank = [ctx.enter_context(nc.psum_tensor(f"bank{i}", [P, 512], f32)) for i in range(8)]
        psS = [bank[0], bank[1]]
        psPT = [bank[2], bank[3]]
        psO = [bank[4], bank[5]]
        psT = [bank[6], bank[7]]
        psG, psV, psY = [bank[0], bank[1]], [bank[2], bank[3]], [bank[4], bank[5]]
        psX, psA = bank[6], bank[7]

        kv_in, aw_in, vec_in, wr_in = sem("kv_in"), sem("aw_in"), sem("vec_in"), sem("wr_in")
        x_in = [sem(f"x_in{h}") for h in range(B)]
        xT_in = [sem(f"xT_in{h}") for h in range(B)]
        bc_in, ew_in = sem("bc_in"), sem("ew_in")
        rows_out, flat_out = sem("rows_out"), sem("flat_out")
        ident0, ident_ok, const_ok, ones_ok, cst_tmp = sem("ident0"), sem("ident_ok"), sem("const_ok"), sem("ones_ok"), sem("cst_tmp")
        k_stats, k_mean, k_cent, kT_tr, kT_ok = sem("k_stats"), sem("k_mean"), sem("k_cent"), sem("kT_tr"), sem("kT_ok")
        w1g_ok, b1_mm, b1_ok, bb_ok = sem("w1g_ok"), sem("b1_mm"), sem("b1_ok"), sem("bb_ok")
        stats_d = [sem(f"stats_d{n}") for n in range(4)]
        mv_ok = [sem(f"mv_ok{n}") for n in range(4)]
        ve_ok = [sem(f"ve_ok{n}") for n in range(4)]
        rstd_ok = [sem(f"rstd_ok{n}") for n in range(4)]
        mr_ok = [sem(f"mr_ok{n}") for n in range(4)]
        nmr_ok = [sem(f"nmr_ok{n}") for n in range(4)]
        r16_ok, q_ok = sem("r16_ok"), sem("q_ok")
        score_mm, mx_ok, nb_ok, exp_ok = sem("score_mm"), sem("mx_ok"), sem("nb_ok"), sem("exp_ok")
        pT_tr, pT_ok, pv_mm, rz_ok, z_ok = sem("pT_tr"), sem("pT_ok"), sem("pv_mm"), sem("rz_ok"), sem("z_ok")
        n_ok, nT_tr, nT_ok, h_mm, h_ok, f_mm = sem("n_ok"), sem("nT_tr"), sem("nT_ok"), sem("h_mm"), sem("h_ok"), sem("f_mm")
        ng_ok, u_ok, xb_ok, v_ok, x1_ok = sem("ng_ok"), sem("u_ok"), sem("xb_ok"), sem("v_ok"), sem("x1_ok")
        flat_ok, fT_tr, fT_ok, lg_mm = sem("flat_ok"), sem("fT_tr"), sem("fT_ok"), sem("lg_mm")
        step = sem("step")
        dm_ok, ex_ok, both_ok, count_mm = sem("dm_ok"), sem("ex_ok"), sem("both_ok"), sem("count_mm")
        ohlo_ok, slots_ok, slot_mm, route_ok = sem("ohlo_ok"), sem("slots_ok"), sem("slot_mm"), sem("route_ok")
        gathered = [sem("gathered0"), sem("gathered1")]
        scattered = sem("scattered")
        X_tr, XT_ok, gate_mm, val_mm = sem("X_tr"), sem("XT_ok"), sem("gate_mm"), sem("val_mm")
        silu_ok, A_ok, A_tr, AT_ok, y_mm, Y_ok = sem("silu_ok"), sem("A_ok"), sem("A_tr"), sem("AT_ok"), sem("y_mm"), sem("Y_ok")

        block = ctx.enter_context(nc.Block())

        def bc(ap, shape):
            return ap.broadcast_to(shape)

        @block.sync
        def _(sp):
            sp.dma_start(kv[:], ctx_kv.rearrange("b u c -> u b c")).then_inc(kv_in, 16)
            for h in range(B):
                ts, cs = slice(h * TH, (h + 1) * TH), slice(h * TH * P, (h + 1) * TH * P)
                sp.dma_start(xs[:, ts, :], x_v[:, ts, :]).then_inc(x_in[h], 16)
                sp.dma_start(xTs[:, :, cs], xT_v[:, :, cs]).then_inc(xT_in[h], 16)
            sp.dma_start(cols[:], vec_cols).then_inc(vec_in, 16)
            sp.dma_start(rows[0:1, 0, :], b2[None, :]).then_inc(vec_in, 16)
            sp.dma_start(rows[0:1, 1, :], beta[None, :]).then_inc(vec_in, 16)
            sp.dma_start(aw1[:], aW1.rearrange("(k p) n -> p k n", p=P)).then_inc(aw_in, 16)
            sp.dma_start(aw2[:], aW2.rearrange("(k p) n -> p k n", p=P)).then_inc(aw_in, 16)
            sp.dma_start(gammaB[:], bc(gamma[None, :], (P, D))).then_inc(bc_in, 16)
            sp.dma_start(betaB[:], bc(beta[None, :], (P, D))).then_inc(bc_in, 16)
            sp.dma_start(wr[:], WrT.rearrange("(k p) e -> p k e", p=P)).then_inc(wr_in, 16)
            sp.wait_ge(const_ok, 1)
            sp.dma_start(out[N:N + P, :], zero[:]).then_inc(rows_out, 16)
            for e in range(E):
                sp.dma_start(W1[:, e, :, :], w1_v[:, e, :, :]).then_inc(ew_in, 16)
                sp.dma_start(W2[:, e, :, :], w2_v[:, e, :, :]).then_inc(ew_in, 16)
            for g in range(NG):
                sp.wait_ge(x1_ok, G * g + G)
                sp.dma_start(out_v[:, bass.ds(G * g, G), :], xs[:, bass.ds(G * g, G), :]).then_inc(rows_out, 16)
                sp.wait_ge(flat_ok, G * g + G)
                sp.dma_start(flat_v[:, bass.ds(G * g, G), :], nf[:, bass.ds(G * g, G), :]).then_inc(flat_out, 16)
            sp.wait_ge(rows_out, 16 * (NG + 1))
            sp.wait_ge(flat_out, 16 * NG)

        @block.gpsimd
        def _(pool):
            nc.gpsimd.memset(ident[:], 0.0).then_inc(ident0, 1)
            nc.gpsimd.memset(zero[:], 0.0).then_inc(const_ok, 1)
            nc.gpsimd.memset(ones_row[:], 1.0).then_inc(ones_ok, 1)
            pool.wait_ge(ident0, 1)
            nc.gpsimd.affine_select(out=ident[:], in_=ident[:], compare_op=ALU.not_equal, fill=1.0, base=0,
                                    pattern=[[-1, P]], channel_multiplier=1).then_inc(ident_ok, 1)
            nc.gpsimd.memset(mhalf[:], -0.5).then_inc(cst_tmp, 1)
            nc.gpsimd.memset(cscale[:], SCALE).then_inc(cst_tmp, 1)
            nc.gpsimd.memset(cneg[:], -1.0).then_inc(cst_tmp, 1)
            nc.gpsimd.memset(epsr[:], 0.0).then_inc(cst_tmp, 1)
            pool.wait_ge(cst_tmp, 4)
            nc.gpsimd.memset(epsr[:, 0, :, 1:2], EPS_IN).then_inc(cst_tmp, 1)
            nc.gpsimd.memset(epsr[:, 1, :, 1:2], EPS_LN).then_inc(cst_tmp, 1)
            pool.wait_ge(cst_tmp, 6)

            def norm(n, g):
                ts = bass.ds(G * g, G)
                pool.wait_ge(mv_ok[n], G * g + G)
                nc.gpsimd.tensor_tensor(ve[:, n, ts, :], mv[:, n, :, :], epsr[:, 1 if n in (1, 2) else 0, :, :],
                                        ALU.add).then_inc(ve_ok[n], 1)
                pool.wait_ge(ve_ok[n], g + 1)
                nc.gpsimd.tensor_tensor(rstd[:, n, ts], ve[:, n, ts, 1], mhalf[:], ALU.pow).then_inc(rstd_ok[n], 1)
                if n == 2:
                    return
                pool.wait_ge(rstd_ok[n], g + 1)
                nc.gpsimd.tensor_tensor(mr[:, n, ts], ve[:, n, ts, 0], rstd[:, n, ts], ALU.mult).then_inc(mr_ok[n], 1)
                if n == 0:
                    nc.gpsimd.tensor_tensor(r16[:, ts], rstd[:, n, ts], cscale[:], ALU.mult).then_inc(r16_ok, 1)
                pool.wait_ge(mr_ok[n], g + 1)
                nc.gpsimd.tensor_tensor(nmr[:, n, ts], mr[:, n, ts], cneg[:], ALU.mult).then_inc(nmr_ok[n], 1)

            with pool.Fori(0, NG) as g:
                norm(0, g)
            pool.wait_ge(bc_in, 32)
            with pool.Fori(0, NG) as g:
                norm(1, g)
                for j in range(G):
                    t = G * g + j
                    pool.wait_ge(n_ok, t + 1)
                    nc.gpsimd.tensor_tensor(zn[:, bass.ds(t, 1), :], nf[:, bass.ds(t, 1), :], gammaB[:, None, :],
                                            ALU.mult).then_inc(ng_ok, 1)
            pool.wait_ge(q_ok, T)
            with pool.Fori(0, NG) as g:
                norm(2, g)
                for j in range(G):
                    t = G * g + j
                    nc.gpsimd.tensor_tensor(xs[:, bass.ds(t, 1), :], xs[:, bass.ds(t, 1), :], betaB[:, None, :],
                                            ALU.add).then_inc(xb_ok, 1)
            with pool.Fori(0, NG) as g:
                norm(3, g)
            nc.gpsimd.memset(onesb[:], 1.0).then_inc(cst_tmp, 1)
            nc.gpsimd.memset(first0[:], 1.0).then_inc(cst_tmp, 1)
            nc.gpsimd.memset(ones8[:], 1.0).then_inc(cst_tmp, 1)
            nc.gpsimd.iota(iota_s[:], [[1, NS]], base=0, channel_multiplier=0,
                           allow_small_or_imprecise_dtypes=True).then_inc(cst_tmp, 1)
            nc.gpsimd.iota(iota_p[:], [[1, P]], base=0, channel_multiplier=0,
                           allow_small_or_imprecise_dtypes=True).then_inc(cst_tmp, 1)
            nc.gpsimd.iota(prio[:], [[-1, E]], base=E, channel_multiplier=0,
                           allow_small_or_imprecise_dtypes=True).then_inc(cst_tmp, 1)
            nc.gpsimd.iota(pairv[:], [[P, Q32]], base=1, channel_multiplier=1,
                           allow_small_or_imprecise_dtypes=True).then_inc(cst_tmp, 1)
            nc.gpsimd.iota(pcol[:], [[N, 2]], base=1, channel_multiplier=1,
                           allow_small_or_imprecise_dtypes=True).then_inc(cst_tmp, 1)
            pool.wait_ge(cst_tmp, 14)
            nc.gpsimd.affine_select(out=tri[:], in_=onesb[:], compare_op=ALU.is_gt, fill=0.0, base=0,
                                    pattern=[[1, P]], channel_multiplier=-1).then_inc(const_ok, 1)
            nc.gpsimd.memset(first0[:, :, 0:1], 0.0).then_inc(const_ok, 1)

            pool.wait_ge(route_ok, 1)
            pool.wait_ge(flat_out, 16 * NG)
            pool.wait_ge(rows_out, 16 * (NG + 1))
            pool.wait_ge(h_ok, KD * NG)
            pool.wait_ge(lg_mm, NG)

            def gather(s):
                if s >= 2:
                    pool.wait_ge(X_tr, s - 1)
                nc.gpsimd.indirect_dma_start(X[:, s % 2, :], None, flat_dram[:, :],
                                             bass.IndirectOffsetOnAxis(gi[:, s:s + 1], 0)).then_inc(gathered[s % 2], 16)

            gather(0)
            gather(1)
            for s in range(NS):
                if s + 2 < NS:
                    gather(s + 2)
                pool.wait_ge(Y_ok, s + 1)
                if s > 0:
                    pool.wait_ge(scattered, 16 * s)
                nc.gpsimd.indirect_dma_start(out[:, :], bass.IndirectOffsetOnAxis(si[:, s:s + 1], 0), Y[:, s % 2, :], None,
                                             compute_op=ALU.add).then_inc(scattered, 16)
            pool.wait_ge(scattered, 16 * NS)

        @block.scalar
        def _(act):
            def normalise(n, g, src, dst, done):
                act.wait_ge(nmr_ok[n], g + 1)
                for j in range(G):
                    t = G * g + j
                    nc.scalar.activation(dst[:, bass.ds(t, 1), :], src[:, bass.ds(t, 1), :], ACT.Identity,
                                         scale=rstd[:, n, bass.ds(t, 1)], bias=nmr[:, n, bass.ds(t, 1)]).then_inc(done, 1)

            act.wait_ge(kT_tr, 1)
            nc.scalar.copy(kT[:], psT[0][:, 0:B * KD * U].rearrange("p (b k u) -> p b k u", b=B, k=KD)).then_inc(kT_ok, 1)
            for h in range(B):
                act.wait_ge(x_in[h], 16)
                with act.Fori(NG // B * h, NG // B * (h + 1)) as g:
                    normalise(0, g, xs, qu, q_ok)
            for h in range(B):
                act.wait_ge(nb_ok, h + 1)
                with act.Fori(0, TH) as j:
                    t = h * TH + j
                    nc.scalar.activation(prob[:, bass.ds(t, 1), :],
                                         psS[h][:, bass.ds(U * j, U)].rearrange("p (a u) -> p a u", a=1), ACT.Exp,
                                         scale=r16[:, bass.ds(t, 1)], bias=nb[:, bass.ds(t, 1)],
                                         accum_out=zsum[:, bass.ds(t, 1)]).then_inc(exp_ok, 1)
                for g in range(NG // B * h, NG // B * (h + 1)):
                    act.wait_ge(pT_tr, g + 1)
                    if g >= 2:
                        act.wait_ge(pv_mm, G // 2 * (g - 1))
                    nc.scalar.copy(probT[:, g % 2, :], psPT[g % 2][0:U, :]).then_inc(pT_ok, 1)

            def transposed(g, r, tr, done, used, first):
                act.wait_ge(tr, g + 1)
                if not first:
                    act.wait_ge(used, 2 * (g - 1) if used is h_mm else g - 1)
                for k in range(KD):
                    nc.scalar.copy(nT[:, r, k, :], psT[k][:]).then_inc(done, 1)

            def relu(g, r, first):
                if not first:
                    act.wait_ge(f_mm, 2 * (g - 1))
                for k in range(KD):
                    act.wait_ge(h_mm, 2 * g + k + 1)
                    nc.scalar.activation(hT[:, r, k, :], psS[k][:], ACT.Relu, bias=b1f[:, k:k + 1]).then_inc(h_ok, 1)

            act.wait_ge(b1_ok, 1)
            act.wait_ge(score_mm, B)
            normalise(1, 0, zn, nf, n_ok)
            for g in range(NG):
                if g + 1 < NG:
                    normalise(1, g + 1, zn, nf, n_ok)
                transposed(g, g % 2, nT_tr, nT_ok, h_mm, g < 2)
                relu(g, g % 2, g < 2)
            act.wait_ge(ng_ok, T)
            act.wait_ge(nT_tr, NG)
            normalise(3, 0, xs, nf, flat_ok)
            for g in range(NG):
                if g + 1 < NG:
                    normalise(3, g + 1, xs, nf, flat_ok)
                transposed(g, g % 2, fT_tr, fT_ok, lg_mm, g < 2)

            act.wait_ge(dm_ok, 1)
            nc.scalar.activation(ex[:], dm[:], ACT.Exp).then_inc(ex_ok, 1)

            act.wait_ge(route_ok, 1)

            def take_xt(s, b, early=False):
                act.wait_ge(X_tr, s + 1)
                if not early:
                    act.wait_ge(val_mm, s - 1)
                nc.scalar.copy(XT[:, b, :, :], psX[:, 0:D].rearrange("p (k n) -> p k n", k=KD)).then_inc(XT_ok, 1)

            def silu(s, b, early=False):
                act.wait_ge(gate_mm, s + 1)
                if not early:
                    act.wait_ge(A_ok, s - 1)
                nc.scalar.activation(S[:, b, :], psG[b][:], ACT.Silu).then_inc(silu_ok, 1)

            def weigh(s, b, early=False):
                act.wait_ge(y_mm, s + 1)
                if not early:
                    act.wait_ge(scattered, 16 * (s - 1))
                nc.scalar.activation(Y[:, b, :], psY[b][:, 0:D], ACT.Copy, scale=slotw[:, bass.ds(s, 1)]).then_inc(Y_ok, 1)

            take_xt(0, 0, True)
            silu(0, 0, True)
            take_xt(1, 1, True)
            silu(1, 1, True)
            take_xt(2, 0)
            weigh(0, 0, True)
            silu(2, 0)
            take_xt(3, 1)
            weigh(1, 1, True)
            with act.Fori(0, (NS - 5) // 2) as i:
                for b in (1, 0):
                    s = 2 * i + 4 - b
                    silu(s, b)
                    take_xt(s + 1, 1 - b)
                    weigh(s - 1, 1 - b)
            silu(NS - 2, 1)
            take_xt(NS - 1, 0)
            weigh(NS - 3, 0)
            silu(NS - 1, 0)
            weigh(NS - 2, 1)
            weigh(NS - 1, 0)

        @block.vector
        def _(dve):
            dve.wait_ge(kv_in, 16)
            for b in range(B):
                nc.vector.bn_stats(kst[:, b, :], kv[:, b, :]).then_inc(k_stats, 1)
            dve.wait_ge(k_stats, B)
            for b in range(B):
                nc.vector.bn_aggr(kmv[:, b, :], kst[:, b, :]).then_inc(k_mean, 1)
            dve.wait_ge(k_mean, B)
            for b in range(B):
                nc.vector.tensor_scalar(kc[:, b, :], kv[:, b, :], kmv[:, b, 0:1], None, ALU.subtract).then_inc(k_cent, 1)

            def norm_stats(n, g, src):
                if n:
                    dve.wait_ge(mv_ok[n - 1], T)
                if g:
                    dve.wait_ge(mv_ok[n], G * g)
                for j in range(G):
                    t = G * g + j
                    nc.vector.bn_stats(st[:, j, :],
                                       src[:, bass.ds(t, 1), :].rearrange("p a c -> p (a c)")).then_inc(stats_d[n], 1)
                dve.wait_ge(stats_d[n], G * g + G)
                if g:
                    dve.wait_ge(ve_ok[n], g)
                for j in range(G):
                    nc.vector.bn_aggr(mv[:, n, j, :], st[:, j, :]).then_inc(mv_ok[n], 1)

            for h in range(B):
                dve.wait_ge(x_in[h], 16)
                for g in range(NG // B * h, NG // B * (h + 1)):
                    norm_stats(0, g, xs)
            for h in range(B):
                hs = slice(h * TH, (h + 1) * TH)
                dve.wait_ge(score_mm, h + 1)
                nc.vector.reduce_max(mx[:, hs], psS[h][:, :].rearrange("p (t u) -> p t u", t=TH), AX.X).then_inc(mx_ok, 1)
                dve.wait_ge(mx_ok, h + 1)
                dve.wait_ge(r16_ok, NG // B * (h + 1))
                nc.vector.scalar_tensor_tensor(out=nb[:, hs], in0=mx[:, hs], scalar=-1.0, in1=r16[:, hs],
                                               op0=ALU.mult, op1=ALU.mult).then_inc(nb_ok, 1)
            dve.wait_ge(aw_in, 32)
            dve.wait_ge(vec_in, 48)
            for k in range(KD):
                nc.vector.tensor_scalar(aw1g[:, k, :], aw1[:, k, :], cols[:, 0, k:k + 1], None, ALU.mult).then_inc(w1g_ok, 1)
            nc.vector.tensor_tensor(bb[:], rows[0:1, 0, :], rows[0:1, 1, :], ALU.add).then_inc(bb_ok, 1)
            dve.wait_ge(b1_mm, 1)
            nc.vector.tensor_tensor(b1f[:], psT[1][:, 0:KD], cols[:, 2, :], ALU.add).then_inc(b1_ok, 1)

            for h in range(B):
                hs = slice(h * TH, (h + 1) * TH)
                dve.wait_ge(exp_ok, TH * (h + 1))
                nc.vector.reciprocal(rz[:, hs], zsum[:, hs]).then_inc(rz_ok, 1)
                dve.wait_ge(rz_ok, h + 1)
                for g in range(NG // B * h, NG // B * (h + 1)):
                    for j in range(G):
                        t = G * g + j
                        dve.wait_ge(q_ok, t + 1)
                        if j % 2 == 0:
                            dve.wait_ge(pv_mm, 2 * g + j // 2 + 1)
                        o = psO[j // 2][:, (j % 2) * D:(j % 2 + 1) * D]
                        nc.vector.scalar_tensor_tensor(out=zn[:, bass.ds(t, 1), :].rearrange("p a c -> p (a c)"), in0=o,
                                                       scalar=rz[:, bass.ds(t, 1)],
                                                       in1=qu[:, bass.ds(t, 1), :].rearrange("p a c -> p (a c)"),
                                                       op0=ALU.mult, op1=ALU.add).then_inc(z_ok, 1)
                    dve.wait_ge(z_ok, G * g + G)
                    norm_stats(1, g, zn)
            for g in range(NG):
                for j in range(G):
                    t = G * g + j
                    dve.wait_ge(ng_ok, t + 1)
                    if j % 2 == 0:
                        dve.wait_ge(f_mm, 2 * g + j // 2 + 1)
                    o = psO[j // 2][:, (j % 2) * D:(j % 2 + 1) * D]
                    nc.vector.tensor_tensor(qu[:, bass.ds(t, 1), :].rearrange("p a c -> p (a c)"), o,
                                            zn[:, bass.ds(t, 1), :].rearrange("p a c -> p (a c)"), ALU.add).then_inc(u_ok, 1)
                dve.wait_ge(u_ok, G * g + G)
                norm_stats(2, g, qu)
            dve.wait_ge(bc_in, 32)
            for g in range(NG):
                dve.wait_ge(rstd_ok[2], g + 1)
                for j in range(G):
                    t = G * g + j
                    u = qu[:, bass.ds(t, 1), :].rearrange("p a c -> p (a c)")
                    nc.vector.scalar_tensor_tensor(out=u, in0=u, scalar=ve[:, 2, bass.ds(t, 1), 0], in1=gammaB[:],
                                                   op0=ALU.subtract, op1=ALU.mult).then_inc(v_ok, 1)
                dve.wait_ge(v_ok, G * g + G)
                for j in range(G):
                    t = G * g + j
                    dve.wait_ge(xb_ok, t + 1)
                    xt1 = xs[:, bass.ds(t, 1), :].rearrange("p a c -> p (a c)")
                    nc.vector.scalar_tensor_tensor(out=xt1, in0=qu[:, bass.ds(t, 1), :].rearrange("p a c -> p (a c)"),
                                                   scalar=rstd[:, 2, bass.ds(t, 1)], in1=xt1,
                                                   op0=ALU.mult, op1=ALU.add).then_inc(x1_ok, 1)
                dve.wait_ge(x1_ok, G * g + G)
                norm_stats(3, g, xs)

            n = [0]

            def link(ins):
                n[0] += 1
                ins.then_inc(step, 1)
                dve.wait_ge(step, n[0])

            v = nc.vector
            TE = (P, T, E)
            dve.wait_ge(lg_mm, NG)
            dve.wait_ge(const_ok, 3)
            link(v.tensor_copy(lg[:], psPT[0][:, 0:T * E].rearrange("p (t e) -> p t e", t=T)))
            prioB = bc(prio[:, None, :], TE)
            for c in range(TOPK):
                src = (lg, lg2)[c]
                link(v.reduce_max(m12[:, c, :], src[:], AX.X))
                link(v.tensor_tensor(pick[:], src[:], bc(m12[:, c, :, None], TE), ALU.is_ge))
                link(v.tensor_tensor(pick[:], pick[:], prioB, ALU.mult))
                link(v.reduce_max(pmax[:, c, :], pick[:], AX.X))
                link(v.tensor_tensor(oh[:, c, :, :], bc(pmax[:, c, :, None], TE), prioB, ALU.is_equal))
                if c == 0:
                    link(v.scalar_tensor_tensor(out=lg2[:], in0=oh[:, 0, :, :], scalar=-3e38, in1=lg[:],
                                                op0=ALU.mult, op1=ALU.add))
            v.tensor_tensor(dm[:], m12[:, 1, :], m12[:, 0, :], ALU.subtract).then_inc(dm_ok, 1)
            v.tensor_tensor(both[:].rearrange("p (t e) -> p t e", t=T), oh[:, 0, :, :], oh[:, 1, :, :], ALU.add).then_inc(both_ok, 1)
            dve.wait_ge(ex_ok, 1)
            link(v.tensor_scalar(den[:], ex[:], 1.0, None, ALU.add))
            link(v.reciprocal(wts[:, 0, :], den[:]))
            link(v.tensor_tensor(wts[:, 1, :], ex[:], wts[:, 0, :], ALU.mult))
            dve.wait_ge(count_mm, 1)
            link(v.tensor_copy(totE[:], psPT[1][:, T * E:2 * T * E].rearrange("p (t e) -> p e t", t=T)))
            link(v.tensor_tensor_scan(incl[:].rearrange("p e t -> p (e t)"), first0[:].rearrange("p e t -> p (e t)"),
                                      totE[:].rearrange("p e t -> p (e t)"), 0.0, ALU.mult, ALU.add))
            v.tensor_scalar(tp[:], incl[:, :, T - 1], float(P - 1), None, ALU.add).then_inc(step, 1)
            n[0] += 1
            link(v.tensor_tensor(excl[:], incl[:], totE[:], ALU.subtract))
            link(v.tensor_scalar(nti[:], tp[:], P.bit_length() - 1, None, ALU.logical_shift_right))
            link(v.tensor_copy(ntf[:], nti[:]))
            link(v.tensor_tensor_scan(ends[:], ones8[:], ntf[:], 0.0, ALU.mult, ALU.add))
            link(v.tensor_tensor(starts[:], ends[:], ntf[:], ALU.subtract))
            link(v.scalar_tensor_tensor(out=base[:], in0=bc(starts[:, None, :], TE), scalar=float(P),
                                        in1=excl[:].rearrange("p e t -> p t e"), op0=ALU.mult, op1=ALU.add))
            link(v.tensor_tensor(rank[:], psPT[1][:, 0:T * E].rearrange("p (t e) -> p t e", t=T), base[:], ALU.add))
            link(v.tensor_tensor(rsel[:], oh[:], bc(rank[:, None, :, :], (P, TOPK, T, E)), ALU.mult))
            link(v.reduce_sum(pos[:].rearrange("p (c t) -> p c t", c=TOPK), rsel[:], AX.X))
            link(v.tensor_copy(posi[:], pos[:]))
            v.tensor_scalar(hii[:], posi[:], P.bit_length() - 1, None, ALU.logical_shift_right).then_inc(step, 1)
            n[0] += 1
            link(v.tensor_scalar(loi[:], posi[:], P - 1, None, ALU.bitwise_and))
            v.tensor_copy(hif[:], hii[:]).then_inc(step, 1)
            n[0] += 1
            link(v.tensor_copy(lof[:], loi[:]))
            with dve.Fori(0, Q32) as q:
                v.tensor_scalar(ohlo[:, bass.ds(q, 1), :].rearrange("p a n -> p (a n)"), iota_p[:], lof[:, bass.ds(q, 1)], None,
                                ALU.is_equal).then_inc(ohlo_ok, 1)
            QS = (P, Q32, NS)
            link(v.tensor_tensor(ohhi[:], bc(iota_s[:, None, :], QS), bc(hif[:, :, None], QS), ALU.is_equal))
            v.tensor_tensor(slots[:, :, 0, :], ohhi[:], bc(pairv[:, :, None], QS), ALU.mult).then_inc(slots_ok, 1)
            v.tensor_tensor(slots[:, :, 1, :], ohhi[:],
                            bc(wts[:].rearrange("p c t -> p (c t)")[:, :, None], QS), ALU.mult).then_inc(slots_ok, 1)
            link(v.tensor_tensor(ge[:], bc(iota_s[0:1, :, None], (1, NS, E)), bc(ends[0:1, None, :], (1, NS, E)), ALU.is_ge))
            link(v.reduce_sum(eidf[:], ge[:], AX.X))
            link(v.tensor_scalar(eid[:], eidf[:], float(E - 1), None, ALU.min))
            dve.wait_ge(slot_mm, 1)
            sval = psPT[0][:, 0:NS]
            v.tensor_copy(slotw[:], psPT[0][:, NS:2 * NS]).then_inc(step, 1)
            v.tensor_scalar(sk[:], sval, N + 0.5, -float(N), ALU.is_gt, ALU.mult).then_inc(step, 1)
            v.tensor_scalar(padg[:], sval, 0.5, pcol[:, 0:1], ALU.is_lt, ALU.mult).then_inc(step, 1)
            n[0] += 3
            link(v.tensor_scalar(pads[:], sval, 0.5, pcol[:, 1:2], ALU.is_lt, ALU.mult))
            link(v.tensor_tensor(stok[:], sk[:], sval, ALU.add))
            v.scalar_tensor_tensor(out=gi[:], in0=padg[:], scalar=-1.0, in1=stok[:], op0=ALU.add, op1=ALU.add).then_inc(step, 1)
            n[0] += 1
            link(v.scalar_tensor_tensor(out=si[:], in0=pads[:], scalar=-1.0, in1=stok[:], op0=ALU.add, op1=ALU.add))
            v.engine_nop().then_inc(route_ok, 1)

            def product(s, b, early=False):
                dve.wait_ge(val_mm, s + 1)
                dve.wait_ge(silu_ok, s + 1)
                if not early:
                    dve.wait_ge(A_tr, s - 1)
                v.tensor_tensor(A[:, b, :], psV[b][:], S[:, b, :], ALU.mult).then_inc(A_ok, 1)

            def take_at(s, first=False):
                dve.wait_ge(A_tr, s + 1)
                if not first:
                    dve.wait_ge(y_mm, s)
                v.tensor_copy(AT[:], psA[:].rearrange("p (k n) -> p k n", k=KF)).then_inc(AT_ok, 1)

            product(0, 0, True)
            take_at(0, True)
            product(1, 1, True)
            take_at(1)
            product(2, 0)
            with dve.Fori(0, (NS - 3) // 2) as i:
                for b in (1, 0):
                    s = 2 * i + 4 - b
                    take_at(s - 1)
                    product(s, b)
            take_at(NS - 1)

        @block.tensor
        def _(pe):
            pe.wait_ge(ident_ok, 1)
            pe.wait_ge(k_cent, B)
            for b in range(B):
                for k in range(KD):
                    c = (b * KD + k) * U
                    last = nc.tensor.transpose(psT[0][:, c:c + U], kc[:, b, k * P:(k + 1) * P], ident[0:U, 0:U])
            last.then_inc(kT_tr, 1)
            pe.wait_ge(kT_ok, 1)
            for h in range(B):
                pe.wait_ge(xT_in[h], 16)
                for j in range(TH):
                    t = h * TH + j
                    for k in range(KD):
                        last = nc.tensor.matmul(psS[h][:, j * U:(j + 1) * U], xTs[:, k, t * P:(t + 1) * P], kT[:, h, k, :],
                                                start=(k == 0), stop=(k == KD - 1))
                last.then_inc(score_mm, 1)
            pe.wait_ge(aw_in, 32)
            pe.wait_ge(vec_in, 48)
            for m in range(KD):
                for k in range(KD):
                    last = nc.tensor.matmul(psT[1][:, m:m + 1], aw1[:, k, m * P:(m + 1) * P], cols[:, 1, k:k + 1],
                                            start=(k == 0), stop=(k == KD - 1))
            last.then_inc(b1_mm, 1)

            def prob_t(g):
                pe.wait_ge(exp_ok, G * g + G)
                if g >= 2:
                    pe.wait_ge(pT_ok, g - 1)
                for j in range(G):
                    last = nc.tensor.transpose(psPT[g % 2][0:U, j * P:(j + 1) * P], prob[:, G * g + j, :], ident[:])
                last.then_inc(pT_tr, 1)

            def pv(g):
                pe.wait_ge(pT_ok, g + 1)
                for j in range(G):
                    if j % 2 == 0 and g > 0:
                        pe.wait_ge(z_ok, G * (g - 1) + j + 2)
                    last = nc.tensor.matmul(psO[j // 2][:, (j % 2) * D:(j % 2 + 1) * D], probT[:, g % 2, j * P:(j + 1) * P],
                                            kv[:, g // (NG // B), :], start=True, stop=True)
                    if j % 2 == 1:
                        last.then_inc(pv_mm, 1)

            prob_t(0)
            for g in range(NG):
                if g + 1 < NG:
                    prob_t(g + 1)
                pv(g)

            def rows_t(g, ok, done, emptied, tr):
                pe.wait_ge(ok, G * g + G)
                if g > 0:
                    pe.wait_ge(emptied, KD * g)
                for k in range(KD):
                    for j in range(G):
                        last = nc.tensor.transpose(psT[k][:, j * P:(j + 1) * P], nf[:, G * g + j, k * P:(k + 1) * P], ident[:])
                last.then_inc(tr, 1)

            def ffn_up(g):
                pe.wait_ge(nT_ok, KD * (g + 1))
                if g == 0:
                    pe.wait_ge(w1g_ok, KD)
                for m in range(KD):
                    if g > 0:
                        pe.wait_ge(h_ok, KD * (g - 1) + m + 1)
                    for k in range(KD):
                        last = nc.tensor.matmul(psS[m][:], aw1g[:, k, m * P:(m + 1) * P], nT[:, g % 2, k, :],
                                                start=(k == 0), stop=(k == KD - 1))
                    last.then_inc(h_mm, 1)

            def ffn_down(g):
                pe.wait_ge(h_ok, KD * (g + 1))
                for j in range(G):
                    if j % 2 == 0:
                        if g == 0:
                            pe.wait_ge(z_ok, G * (NG - 1) + j + 2)
                        else:
                            pe.wait_ge(u_ok, G * (g - 1) + j + 2)
                    o = psO[j // 2][:, (j % 2) * D:(j % 2 + 1) * D]
                    for k in range(KD):
                        nc.tensor.matmul(o, hT[:, g % 2, k, j * P:(j + 1) * P], aw2[:, k, :], start=(k == 0), stop=False)
                    last = nc.tensor.matmul(o, ones_row[:], bb[:], start=False, stop=True)
                    if j % 2 == 1:
                        last.then_inc(f_mm, 1)

            pe.wait_ge(bb_ok, 1)
            pe.wait_ge(ones_ok, 1)
            pe.wait_ge(b1_ok, 1)
            rows_t(0, n_ok, nT_ok, nT_ok, nT_tr)
            for g in range(NG):
                ffn_up(g)
                if g + 1 < NG:
                    rows_t(g + 1, n_ok, nT_ok, nT_ok, nT_tr)
                ffn_down(g)

            def logits(g):
                pe.wait_ge(fT_ok, KD * (g + 1))
                for j in range(G):
                    t = G * g + j
                    for k in range(KD):
                        last = nc.tensor.matmul(psPT[0][:, t * E:(t + 1) * E], nT[:, g % 2, k, j * P:(j + 1) * P], wr[:, k, :],
                                                start=(k == 0), stop=(k == KD - 1))
                last.then_inc(lg_mm, 1)

            pe.wait_ge(wr_in, 16)
            pe.wait_ge(nT_ok, KD * NG)
            for g in range(NG):
                rows_t(g, flat_ok, fT_ok, fT_ok, fT_tr)
                if g > 0:
                    logits(g - 1)
            logits(NG - 1)
            pe.wait_ge(both_ok, 1)
            nc.tensor.matmul(psPT[1][:, 0:T * E], tri[:], both[:], start=True, stop=True)
            nc.tensor.matmul(psPT[1][:, T * E:2 * T * E], onesb[:], both[:], start=True, stop=True).then_inc(count_mm, 1)
            pe.wait_ge(slots_ok, 2)
            pe.wait_ge(ohlo_ok, Q32)
            for q in range(Q32):
                last = nc.tensor.matmul(psPT[0][:, 0:2 * NS], ohlo[:, q, :], slots[:, q, :, :].rearrange("p a s -> p (a s)"),
                                        start=(q == 0), stop=(q == Q32 - 1))
            last.then_inc(slot_mm, 1)

            pe.wait_ge(route_ok, 1)
            pe.wait_ge(ew_in, 32 * E)

            def expert(s):
                return pe.value_load(eid[0:1, bass.ds(s, 1)], min_val=0, max_val=E - 1)

            def w1_at(e, k, h):
                return W1[:, bass.ds(e, 1), k, h * F:(h + 1) * F].rearrange("p a f -> p (a f)")

            def rows_in(s, b, n, first=False):
                pe.wait_ge(gathered[b], 16 * n)
                if not first:
                    pe.wait_ge(XT_ok, s)
                for k in range(KD):
                    last = nc.tensor.transpose(psX[:, k * P:(k + 1) * P], X[:, b, k * P:(k + 1) * P], ident[:])
                last.then_inc(X_tr, 1)

            def gate(s, b, e, early=False):
                pe.wait_ge(XT_ok, s + 1)
                if not early:
                    pe.wait_ge(silu_ok, s - 1)
                for k in range(KD):
                    last = nc.tensor.matmul(psG[b][:], XT[:, b, k, :], w1_at(e, k, 1), start=(k == 0), stop=(k == KD - 1))
                last.then_inc(gate_mm, 1)

            def val(s, b, e, early=False):
                if not early:
                    pe.wait_ge(A_ok, s - 1)
                for k in range(KD):
                    last = nc.tensor.matmul(psV[b][:], XT[:, b, k, :], w1_at(e, k, 0), start=(k == 0), stop=(k == KD - 1))
                last.then_inc(val_mm, 1)

            def act_t(s, b, first=False):
                pe.wait_ge(A_ok, s + 1)
                if not first:
                    pe.wait_ge(AT_ok, s)
                for k in range(KF):
                    last = nc.tensor.transpose(psA[:, k * P:(k + 1) * P], A[:, b, k * P:(k + 1) * P], ident[:])
                last.then_inc(A_tr, 1)

            def down(s, b, e, early=False):
                pe.wait_ge(AT_ok, s + 1)
                if not early:
                    pe.wait_ge(Y_ok, s - 1)
                for k in range(KF):
                    last = nc.tensor.matmul(psY[b][:, 0:D], AT[:, k, :],
                                            W2[:, bass.ds(e, 1), k, :].rearrange("p a c -> p (a c)"),
                                            start=(k == 0), stop=(k == KF - 1))
                last.then_inc(y_mm, 1)

            rows_in(0, 0, 1, True)
            e = expert(0)
            gate(0, 0, e, True)
            val(0, 0, e, True)
            rows_in(1, 1, 1)
            e = expert(1)
            gate(1, 1, e, True)
            act_t(0, 0, True)
            val(1, 1, e, True)
            rows_in(2, 0, 2)
            down(0, 0, expert(0), True)
            e = expert(2)
            gate(2, 0, e)
            act_t(1, 1)
            val(2, 0, e)
            rows_in(3, 1, 2)
            down(1, 1, expert(1), True)
            with pe.Fori(0, (NS - 5) // 2) as i:
                for b in (1, 0):
                    s = 2 * i + 4 - b
                    e = expert(s)
                    gate(s, b, e)
                    act_t(s - 1, 1 - b)
                    val(s, b, e)
                    rows_in(s + 1, 1 - b, i + 3)
                    down(s - 1, 1 - b, expert(s - 1))
            for s in (NS - 2, NS - 1):
                b = s % 2
                e = expert(s)
                gate(s, b, e)
                act_t(s - 1, 1 - b)
                val(s, b, e)
                if s + 1 < NS:
                    rows_in(s + 1, 1 - b, (NS + 1) // 2)
                down(s - 1, 1 - b, expert(s - 1))
            act_t(NS - 1, 0)
            down(NS - 1, 0, expert(NS - 1))


def kernel(x, ctx_1024, L0_xattn_W1, L0_xattn_b1, L0_xattn_W2, L0_xattn_b2, L0_xattn_gamma, L0_xattn_beta,
           L0_ffn_Wr, L0_ffn_W1, L0_ffn_W2):
    import numpy as np
    import concourse.bacc as bacc
    from concourse import mybir
    from concourse.bass_utils import run_bass_kernel_spmd

    x = np.asarray(x)
    Bb, R, D = x.shape
    N = Bb * R
    flat = np.ascontiguousarray(x.reshape(N, D))
    ins = {
        "x": flat,
        "xT": np.ascontiguousarray(flat.T),
        "ctx_kv": np.ascontiguousarray(ctx_1024),
        "aW1": np.ascontiguousarray(L0_xattn_W1),
        "aW2": np.ascontiguousarray(L0_xattn_W2),
        "vec_cols": np.ascontiguousarray(np.stack([L0_xattn_gamma, L0_xattn_beta, L0_xattn_b1])
                                         .reshape(3, D // 128, 128).transpose(2, 0, 1)),
        "b2": np.ascontiguousarray(L0_xattn_b2),
        "gamma": np.ascontiguousarray(L0_xattn_gamma),
        "beta": np.ascontiguousarray(L0_xattn_beta),
        "WrT": np.ascontiguousarray(np.asarray(L0_ffn_Wr).T),
        "eW1": np.ascontiguousarray(np.asarray(L0_ffn_W1).transpose(0, 2, 1)),
        "eW2": np.ascontiguousarray(np.asarray(L0_ffn_W2).transpose(0, 2, 1)),
    }
    nc = bacc.Bacc("TRN2", target_bir_lowering=False, num_devices=1)
    aps = [nc.dram_tensor(f"in_{k}", v.shape, mybir.dt.from_np(v.dtype), kind="ExternalInput").ap() for k, v in ins.items()]
    flat_dram = nc.dram_tensor("flat_rows", (N, D), mybir.dt.float32, kind="Internal").ap()
    out = nc.dram_tensor("out_rows", (N + 128, D), mybir.dt.float32, kind="ExternalOutput").ap()
    xattn_then_sparse_experts(nc, *aps, flat_dram, out)
    r = run_bass_kernel_spmd(nc, [{f"in_{k}": v for k, v in ins.items()}], core_ids=[0])
    return r.results[0]["out_rows"][:N].reshape(Bb, R, D)
```

```python
import concourse.bass as bass
from concourse import mybir
from contextlib import ExitStack


def xattn_then_sparse_experts(nc, x, xT, ctx_kv, aW1, aW2, vec_cols, b2, gamma, beta, WrT, eW1, eW2, flat_dram, out):
    f32, bf16, i32 = mybir.dt.float32, mybir.dt.bfloat16, mybir.dt.int32
    ACT = mybir.ActivationFunctionType
    ALU = mybir.AluOpType
    AX = mybir.AxisListType

    P = 128
    N, D = x.shape
    B, U, _ = ctx_kv.shape
    E, _, F2 = eW1.shape
    F = F2 // 2
    KD = D // P
    KF = F // P
    T = N // P
    G = 4
    NG = T // G
    TH = T // B
    TOPK = 2
    Q32 = TOPK * T
    NS = TOPK * T + E - 1
    SCALE = 1.0 / 16.0
    EPS_IN, EPS_LN = 1e-5, 1e-6
    assert D == 256 and NS % 4 == 3

    x_v = x.rearrange("(t p) c -> p t c", p=P)
    xT_v = xT.rearrange("(k p) n -> p k n", p=P)
    out_v = out[0:N, :].rearrange("(t p) c -> p t c", p=P)
    flat_v = flat_dram.rearrange("(t p) c -> p t c", p=P)
    w1_v = eW1.rearrange("e (k p) f -> p e k f", p=P)
    w2_v = eW2.rearrange("e (k p) c -> p e k c", p=P)

    ctx = ExitStack()
    with ctx:
        def sb(name, shape, dt=f32):
            return ctx.enter_context(nc.sbuf_tensor(name, shape, dt))

        def sem(name):
            return ctx.enter_context(nc.semaphore(name))

        W1 = sb("expert_w1", [P, E, KD, F2])
        W2 = sb("expert_w2", [P, E, KF, D])
        xs = sb("xs", [P, T, D])
        qu = sb("qu", [P, T, D])
        zn = sb("zn", [P, 2 * G, D])
        nf = sb("nf", [P, 2 * G, D])
        xt_area = sb("xt_area", [P, KD * N])
        xTs = xt_area[:, :].rearrange("p (k n) -> p k n", k=KD)
        nT = sb("nT", [P, KD, G * P])
        hT = sb("hT", [P, KD, G * P])
        prob = sb("prob", [P, G, U])
        probT = sb("probT", [U, G * P])
        kv = sb("kv", [U, B, D])
        kc = sb("kc", [U, B, D])
        kT = sb("kT", [P, KD, B * U])
        aw1 = sb("aw1", [P, KD, D])
        aw1g = sb("aw1g", [P, KD, D])
        aw2 = sb("aw2", [P, KD, D])
        wr = sb("wr", [P, KD, P])
        cols = sb("cols", [P, 3, KD])
        b1f = sb("b1f", [P, KD])
        rows = sb("rows", [1, 2, D])
        bb = sb("bb", [1, 3, D])
        bbp = sb("bbp", [1, 3, D], bf16)
        bb3 = sb("bb3", [3, D], bf16)
        ones3 = sb("ones3", [3, P], bf16)
        gammaB = sb("gammaB", [P, D])
        betaB = sb("betaB", [P, D])
        ident = sb("ident", [P, P])
        zero = sb("zero", [P, D])
        epsr = sb("epsr", [P, 2, G, 2])
        mhalf = sb("mhalf", [P, G])
        cscale = sb("cscale", [P, G])
        cneg = sb("cneg", [P, G])
        kst = sb("kst", [U, B, 6])
        kmv = sb("kmv", [U, B, 2])
        st = sb("st", [P, 4, G, 6])
        mv = sb("mv", [P, 4, G, 2])
        ve = sb("ve", [P, 4, T, 2])
        rstd = sb("rstd", [P, 4, T])
        mr = sb("mr", [P, 4, T])
        nmr = sb("nmr", [P, 4, T])
        r16 = sb("r16", [P, T])
        mx = sb("mx", [P, T])
        nb = sb("nb", [P, T])
        zsum = sb("zsum", [P, T])
        rz = sb("rz", [P, T])
        wts = sb("wts", [P, TOPK, T])
        prio = sb("prio", [P, E])
        tri = sb("tri", [P, P], bf16)
        onesb = sb("onesb", [P, P], bf16)
        first0 = sb("first0", [P, E, T])
        ones8 = sb("ones8", [P, E])
        iota_s = sb("iota_s", [P, NS])
        iota_p = sb("iota_p", [P, P])
        pairv = sb("pairv", [P, Q32])
        pcol = sb("pcol", [P, 2])
        eid = sb("eid", [1, NS], i32)
        slotw = sb("slotw", [P, NS])
        gi = sb("gi", [P, NS], i32)
        si = sb("si", [P, NS], i32)
        both = sb("both", [P, T * E], bf16)

        free = {"zn": 0, "nf": 0}
        zn_flat = zn[:, :, :].rearrange("p t c -> p (t c)")
        nf_flat = nf[:, :, :].rearrange("p t c -> p (t c)")

        def scratch(where, *dims):
            size = 1
            for d in dims:
                size *= d
            src = zn_flat if where == "zn" else nf_flat
            ap = src[:, free[where]:free[where] + size]
            free[where] += size
            names = "abc"[:len(dims)]
            if len(dims) == 1:
                return ap
            return ap.rearrange(f"p ({' '.join(names)}) -> p {' '.join(names)}", **dict(zip(names, dims)))

        lg = sb("lg", [P, T, E])
        lg2, pick = scratch("zn", T, E), scratch("zn", T, E)
        oh = scratch("zn", TOPK, T * E).rearrange("p c (t e) -> p c t e", t=T)
        rsel = scratch("nf", TOPK, T * E).rearrange("p c (t e) -> p c t e", t=T)
        totE, incl, excl = scratch("zn", E, T), scratch("zn", E, T), scratch("zn", E, T)
        base, rank = scratch("zn", T, E), scratch("zn", T, E)
        m12, pmax = scratch("zn", TOPK, T), scratch("zn", TOPK, T)
        dm, ex, den = scratch("zn", T), scratch("zn", T), scratch("zn", T)
        pos, hif, lof = scratch("zn", Q32), scratch("zn", Q32), scratch("zn", Q32)
        posi, hii, loi = (scratch("zn", Q32).bitcast(i32) for _ in range(3))
        ntf, ends, starts = scratch("nf", E), scratch("nf", E), scratch("nf", E)
        tp, nti = scratch("nf", E).bitcast(i32), scratch("nf", E).bitcast(i32)
        ge = scratch("nf", NS, E)[0:1]
        eidf = scratch("nf", NS)[0:1]
        sk, stok, padg, pads = (scratch("nf", NS) for _ in range(4))
        assert free["zn"] <= 2 * G * D and free["nf"] <= 2 * G * D
        ohlo = xt_area[:, :].rearrange("p (q n) -> p q n", q=Q32)
        slots = qu[:, :, :].rearrange("p t c -> p (t c)")[:, 0:Q32 * 3 * NS].rearrange(
            "p (q a s) -> p q a s", q=Q32, a=3)

        at = [0]

        def area(n):
            at[0] += n
            return xt_area[:, at[0] - n:at[0]]

        NX = 4
        X = zn_flat[:, 0:NX * D].rearrange("p (b c) -> p b c", b=NX)
        XT = area(2 * D).rearrange("p (b k n) -> p b k n", b=2, k=KD)
        S = area(2 * F).rearrange("p (b f) -> p b f", b=2)
        A = area(2 * F).rearrange("p (b f) -> p b f", b=2)
        AT = area(F).rearrange("p (k n) -> p k n", k=KF)
        Y = area(2 * D).rearrange("p (b c) -> p b c", b=2)

        bank = [ctx.enter_context(nc.psum_tensor(f"bank{i}", [P, 512], f32)) for i in range(8)]
        psH = [bank[0], bank[1]]
        psS, psPT = bank[2], bank[3]
        psO = [bank[4], bank[5]]
        psT = [bank[6], bank[7]]
        psG, psV, psY = [bank[0], bank[1]], [bank[2], bank[3]], [bank[4], bank[5]]
        psX, psA = bank[6], bank[7]
        psC, psR = bank[2], bank[3]

        kv_in, aw_in, vec_in, wr_in = sem("kv_in"), sem("aw_in"), sem("vec_in"), sem("wr_in")
        x_in = [sem(f"x_in{g}") for g in range(NG)]
        xT_in = [sem(f"xT_in{g}") for g in range(NG)]
        bc_in, ew_in = sem("bc_in"), sem("ew_in")
        rows_out, bb3_in = sem("rows_out"), sem("bb3_in")
        flat_out = [sem(f"flat_out{g}") for g in range(NG)]
        ident0, ident_ok, zero_ok, ones3_ok, wr0 = sem("ident0"), sem("ident_ok"), sem("zero_ok"), sem("ones3_ok"), sem("wr0")
        cst_tmp, const_ok = sem("cst_tmp"), sem("const_ok")
        k_stats, k_mean, k_cent, kT_tr, kT_ok = sem("k_stats"), sem("k_mean"), sem("k_cent"), sem("kT_tr"), sem("kT_ok")
        w1g_ok, b1_mm, b1_ok, bb_d, bb_ok = sem("w1g_ok"), sem("b1_mm"), sem("b1_ok"), sem("bb_d"), sem("bb_ok")
        stats_d = [sem(f"stats_d{n}") for n in range(4)]
        mv_ok = [sem(f"mv_ok{n}") for n in range(4)]
        ve_ok = [sem(f"ve_ok{n}") for n in range(4)]
        rstd_ok = [sem(f"rstd_ok{n}") for n in range(4)]
        mr_ok = [sem(f"mr_ok{n}") for n in range(4)]
        nmr_ok = [sem(f"nmr_ok{n}") for n in range(4)]
        r16_ok, q_ok = sem("r16_ok"), sem("q_ok")
        score_mm, mx_ok, nb_ok, exp_ok = sem("score_mm"), sem("mx_ok"), sem("nb_ok"), sem("exp_ok")
        pT_tr, pT_ok, pv_mm, rz_ok, z_ok = sem("pT_tr"), sem("pT_ok"), sem("pv_mm"), sem("rz_ok"), sem("z_ok")
        n_ok, nT_tr, nT_ok, h_mm, h_ok, f_mm = sem("n_ok"), sem("nT_tr"), sem("nT_ok"), sem("h_mm"), sem("h_ok"), sem("f_mm")
        ng_ok, u_ok, xb_ok, v_ok, x1_ok = sem("ng_ok"), sem("u_ok"), sem("xb_ok"), sem("v_ok"), sem("x1_ok")
        flat_ok, fT_tr, fT_ok, lg_mm, lg_ok = sem("flat_ok"), sem("fT_tr"), sem("fT_ok"), sem("lg_mm"), sem("lg_ok")
        step = sem("step")
        ohhi_ok, slotsw_ok = sem("ohhi_ok"), sem("slotsw_ok")
        dm_ok, ex_ok, both_ok, count_mm = sem("dm_ok"), sem("ex_ok"), sem("both_ok"), sem("count_mm")
        ohlo_ok, slots_ok, slot_mm, route_ok = sem("ohlo_ok"), sem("slots_ok"), sem("slot_mm"), sem("route_ok")
        gathered = [sem(f"gathered{b}") for b in range(NX)]
        scattered = sem("scattered")
        X_tr, XT_ok, gate_mm, val_mm = sem("X_tr"), sem("XT_ok"), sem("gate_mm"), sem("val_mm")
        silu_ok, A_ok, A_tr, AT_ok, y_mm, Y_ok = sem("silu_ok"), sem("A_ok"), sem("A_tr"), sem("AT_ok"), sem("y_mm"), sem("Y_ok")

        block = ctx.enter_context(nc.Block())

        def bc(ap, shape):
            return ap.broadcast_to(shape)

        @block.sync
        def _(sp):
            sp.dma_start(kv[:], ctx_kv.rearrange("b u c -> u b c")).then_inc(kv_in, 16)
            def load_rows(g):
                ts, cs = slice(g * G, (g + 1) * G), slice(g * G * P, (g + 1) * G * P)
                sp.dma_start(xs[:, ts, :], x_v[:, ts, :]).then_inc(x_in[g], 16)
                sp.dma_start(xTs[:, :, cs], xT_v[:, :, cs]).then_inc(xT_in[g], 16)

            load_rows(0)
            load_rows(1)
            sp.dma_start(cols[:], vec_cols).then_inc(vec_in, 16)
            sp.dma_start(rows[0:1, 0, :], b2[None, :]).then_inc(vec_in, 16)
            sp.dma_start(rows[0:1, 1, :], beta[None, :]).then_inc(vec_in, 16)
            sp.dma_start(aw1[:], aW1.rearrange("(k p) n -> p k n", p=P)).then_inc(aw_in, 16)
            sp.dma_start(aw2[:], aW2.rearrange("(k p) n -> p k n", p=P)).then_inc(aw_in, 16)
            sp.dma_start(gammaB[:], bc(gamma[None, :], (P, D))).then_inc(bc_in, 16)
            sp.dma_start(betaB[:], bc(beta[None, :], (P, D))).then_inc(bc_in, 16)
            load_rows(2)
            load_rows(3)
            sp.wait_ge(wr0, 1)
            sp.dma_start(wr[:, :, 0:E], WrT.rearrange("(k p) e -> p k e", p=P)).then_inc(wr_in, 16)
            sp.wait_ge(zero_ok, 1)
            sp.dma_start(out[N:N + P, :], zero[:]).then_inc(rows_out, 16)
            sp.wait_ge(bb_ok, 1)
            for a in range(3):
                sp.dma_start(bb3[a:a + 1, :], bbp[0:1, a, :]).then_inc(bb3_in, 16)
            for e in range(E):
                sp.dma_start(W1[:, e, :, :], w1_v[:, e, :, :]).then_inc(ew_in, 16)
                sp.dma_start(W2[:, e, :, :], w2_v[:, e, :, :]).then_inc(ew_in, 16)
            for g in range(NG):
                ts, rs = slice(G * g, G * g + G), slice(G * (g % 2), G * (g % 2) + G)
                sp.wait_ge(x1_ok, G * g + G)
                sp.dma_start(out_v[:, ts, :], xs[:, ts, :]).then_inc(rows_out, 16)
                sp.wait_ge(flat_ok, G * g + G)
                sp.dma_start(flat_v[:, ts, :], nf[:, rs, :]).then_inc(flat_out[g], 16)
            sp.wait_ge(rows_out, 16 * (NG + 1))
            for g in range(NG):
                sp.wait_ge(flat_out[g], 16)

        @block.gpsimd
        def _(pool):
            nc.gpsimd.memset(ident[:], 0.0).then_inc(ident0, 1)
            nc.gpsimd.memset(wr[:], 0.0).then_inc(wr0, 1)
            pool.wait_ge(ident0, 1)
            nc.gpsimd.affine_select(out=ident[:], in_=ident[:], compare_op=ALU.not_equal, fill=1.0, base=0,
                                    pattern=[[-1, P]], channel_multiplier=1).then_inc(ident_ok, 1)
            nc.gpsimd.memset(mhalf[:], -0.5).then_inc(cst_tmp, 1)
            nc.gpsimd.memset(cscale[:], SCALE).then_inc(cst_tmp, 1)
            nc.gpsimd.memset(cneg[:], -1.0).then_inc(cst_tmp, 1)
            nc.gpsimd.memset(epsr[:], 0.0).then_inc(cst_tmp, 1)
            pool.wait_ge(cst_tmp, 4)
            nc.gpsimd.memset(epsr[:, 0, :, 1:2], EPS_IN).then_inc(cst_tmp, 1)
            nc.gpsimd.memset(epsr[:, 1, :, 1:2], EPS_LN).then_inc(cst_tmp, 1)
            pool.wait_ge(cst_tmp, 6)

            def norm(n, g):
                ts = slice(G * g, G * g + G)
                pool.wait_ge(mv_ok[n], G * g + G)
                nc.gpsimd.tensor_tensor(ve[:, n, ts, :], mv[:, n, :, :], epsr[:, 1 if n in (1, 2) else 0, :, :],
                                        ALU.add).then_inc(ve_ok[n], 1)
                pool.wait_ge(ve_ok[n], g + 1)
                nc.gpsimd.tensor_tensor(rstd[:, n, ts], ve[:, n, ts, 1], mhalf[:], ALU.pow).then_inc(rstd_ok[n], 1)
                if n == 2:
                    return
                pool.wait_ge(rstd_ok[n], g + 1)
                nc.gpsimd.tensor_tensor(mr[:, n, ts], ve[:, n, ts, 0], rstd[:, n, ts], ALU.mult).then_inc(mr_ok[n], 1)
                if n == 0:
                    nc.gpsimd.tensor_tensor(r16[:, ts], rstd[:, n, ts], cscale[:], ALU.mult).then_inc(r16_ok, 1)
                pool.wait_ge(mr_ok[n], g + 1)
                nc.gpsimd.tensor_tensor(nmr[:, n, ts], mr[:, n, ts], cneg[:], ALU.mult).then_inc(nmr_ok[n], 1)

            def gamma_n(g):
                for j in range(G):
                    r = G * (g % 2) + j
                    pool.wait_ge(n_ok, G * g + j + 1)
                    nc.gpsimd.tensor_tensor(zn[:, r, :], nf[:, r, :], gammaB[:], ALU.mult).then_inc(ng_ok, 1)

            def x_beta(g):
                pool.wait_ge(q_ok, G * g + G)
                for t in range(G * g, G * g + G):
                    nc.gpsimd.tensor_tensor(xs[:, t, :], xs[:, t, :], betaB[:], ALU.add).then_inc(xb_ok, 1)

            for g in range(NG):
                norm(0, g)
                if g == 0:
                    nc.gpsimd.memset(ones3[:], 1.0).then_inc(ones3_ok, 1)
                    nc.gpsimd.memset(zero[:], 0.0).then_inc(zero_ok, 1)
            pool.wait_ge(bc_in, 32)
            for i in range(NG + 1):
                if i < NG:
                    x_beta(i)
                    norm(1, i)
                if i > 0:
                    norm(2, i - 1)
                if i < NG:
                    gamma_n(i)
                if i == 0:
                    nc.gpsimd.memset(onesb[:], 1.0).then_inc(cst_tmp, 1)
                    nc.gpsimd.memset(first0[:], 1.0).then_inc(cst_tmp, 1)
                    nc.gpsimd.memset(ones8[:], 1.0).then_inc(cst_tmp, 1)
                    nc.gpsimd.iota(iota_s[:], [[1, NS]], base=0, channel_multiplier=0,
                                   allow_small_or_imprecise_dtypes=True).then_inc(cst_tmp, 1)
                    nc.gpsimd.iota(iota_p[:], [[1, P]], base=0, channel_multiplier=0,
                                   allow_small_or_imprecise_dtypes=True).then_inc(cst_tmp, 1)
                    nc.gpsimd.iota(prio[:], [[-1, E]], base=E, channel_multiplier=0,
                                   allow_small_or_imprecise_dtypes=True).then_inc(cst_tmp, 1)
                    nc.gpsimd.iota(pairv[:], [[P, Q32]], base=1, channel_multiplier=1,
                                   allow_small_or_imprecise_dtypes=True).then_inc(cst_tmp, 1)
                    nc.gpsimd.iota(pcol[:], [[N, 2]], base=1, channel_multiplier=1,
                                   allow_small_or_imprecise_dtypes=True).then_inc(cst_tmp, 1)
                    pool.wait_ge(cst_tmp, 14)
                    nc.gpsimd.affine_select(out=tri[:], in_=onesb[:], compare_op=ALU.is_gt, fill=0.0, base=0,
                                            pattern=[[1, P]], channel_multiplier=-1).then_inc(const_ok, 1)
                    nc.gpsimd.memset(first0[:, :, 0:1], 0.0).then_inc(const_ok, 1)
                else:
                    norm(3, i - 1)

            pool.wait_ge(ohhi_ok, 1)
            nc.gpsimd.tensor_tensor(slots[:, :, 1, :], slots[:, :, 2, :],
                                    bc(wts[:].rearrange("p c t -> p (c t)")[:, :, None], (P, Q32, NS)),
                                    ALU.mult).then_inc(slotsw_ok, 1)

            pool.wait_ge(route_ok, 1)
            for g in range(NG):
                pool.wait_ge(flat_out[g], 16)
            pool.wait_ge(rows_out, 16 * (NG + 1))

            def gather(s):
                if s >= NX:
                    pool.wait_ge(X_tr, s - NX + 1)
                nc.gpsimd.indirect_dma_start(X[:, s % NX, :], None, flat_dram[:, :],
                                             bass.IndirectOffsetOnAxis(gi[:, s:s + 1], 0)).then_inc(gathered[s % NX], 16)

            for s in range(NX - 1):
                gather(s)
            for s in range(NS):
                if s + NX - 1 < NS:
                    gather(s + NX - 1)
                pool.wait_ge(Y_ok, s + 1)
                if s > 0:
                    pool.wait_ge(scattered, 16 * s)
                nc.gpsimd.indirect_dma_start(out[:, :], bass.IndirectOffsetOnAxis(si[:, s:s + 1], 0), Y[:, s % 2, :], None,
                                             compute_op=ALU.add).then_inc(scattered, 16)
            pool.wait_ge(scattered, 16 * NS)

        @block.scalar
        def _(act):
            def normalise(n, src, s0, dst, d0, g, done):
                act.wait_ge(nmr_ok[n], g + 1)
                for j in range(G):
                    t = G * g + j
                    nc.scalar.activation(dst[:, d0 + j, :], src[:, s0 + j, :], ACT.Identity,
                                         scale=rstd[:, n, t:t + 1], bias=nmr[:, n, t:t + 1]).then_inc(done, 1)

            def queries(g):
                act.wait_ge(x_in[g], 16)
                normalise(0, xs, G * g, qu, G * g, g, q_ok)

            def exponentials(g):
                act.wait_ge(nb_ok, g + 1)
                if g > 0:
                    act.wait_ge(pT_tr, g)
                b = g // (NG // B)
                for j in range(G):
                    t = G * g + j
                    nc.scalar.activation(prob[:, j, :], psS[:, j * B * U + b * U:j * B * U + (b + 1) * U], ACT.Exp,
                                         scale=r16[:, t:t + 1], bias=nb[:, t:t + 1],
                                         accum_out=zsum[:, t:t + 1]).then_inc(exp_ok, 1)

            def take_prob_t(g):
                act.wait_ge(pT_tr, g + 1)
                if g > 0:
                    act.wait_ge(pv_mm, 2 * g)
                nc.scalar.copy(probT[:], psPT[0:U, :]).then_inc(pT_ok, 1)

            def attention_rows(g):
                if g >= 2:
                    act.wait_ge(flat_out[g - 2], 16)
                    act.wait_ge(fT_tr, g - 1)
                normalise(1, zn, G * (g % 2), nf, G * (g % 2), g, n_ok)

            def take_n_t(g):
                act.wait_ge(nT_tr, g + 1)
                if g >= 1:
                    act.wait_ge(h_mm, KD * g)
                if g >= 2:
                    act.wait_ge(lg_mm, g - 1)
                for k in range(KD):
                    nc.scalar.copy(nT[:, k, :], psT[k][:]).then_inc(nT_ok, 1)

            def relu(g):
                if g == 0:
                    act.wait_ge(b1_ok, 1)
                else:
                    act.wait_ge(f_mm, 2 * g)
                for k in range(KD):
                    act.wait_ge(h_mm, KD * g + k + 1)
                    nc.scalar.activation(hT[:, k, :], psH[k][:], ACT.Relu, bias=b1f[:, k:k + 1]).then_inc(h_ok, 1)

            def expert_rows(g):
                act.wait_ge(nT_tr, g + 1)
                act.wait_ge(ng_ok, G * g + G)
                normalise(3, xs, G * g, nf, G * (g % 2), g, flat_ok)

            def take_f_t(g):
                act.wait_ge(fT_tr, g + 1)
                if g + 1 < NG:
                    act.wait_ge(h_mm, KD * (g + 2))
                else:
                    act.wait_ge(lg_mm, NG - 1)
                for k in range(KD):
                    nc.scalar.copy(nT[:, k, :], psT[k][:]).then_inc(fT_ok, 1)

            act.wait_ge(kT_tr, 1)
            nc.scalar.copy(kT[:], psT[0][:, 0:B * KD * U].rearrange("p (k n) -> p k n", k=KD)).then_inc(kT_ok, 1)
            queries(0)
            exponentials(0)
            for i in range(NG + 2):
                if 1 <= i <= NG:
                    take_n_t(i - 1)
                if i < NG:
                    take_prob_t(i)
                if 1 <= i <= NG:
                    relu(i - 1)
                if i + 1 < NG:
                    queries(i + 1)
                if i >= 2:
                    expert_rows(i - 2)
                    take_f_t(i - 2)
                if i < NG:
                    attention_rows(i)
                if i + 1 < NG:
                    exponentials(i + 1)

            act.wait_ge(dm_ok, 1)
            nc.scalar.activation(ex[:], dm[:], ACT.Exp).then_inc(ex_ok, 1)

            act.wait_ge(route_ok, 1)

            def take_xt(s, b, early=False):
                act.wait_ge(X_tr, s + 1)
                if not early:
                    act.wait_ge(val_mm, s - 1)
                nc.scalar.copy(XT[:, b, :, :], psX[:, 0:D].rearrange("p (k n) -> p k n", k=KD)).then_inc(XT_ok, 1)

            def silu(s, b, early=False):
                act.wait_ge(gate_mm, s + 1)
                if not early:
                    act.wait_ge(A_ok, s - 1)
                nc.scalar.activation(S[:, b, :], psG[b][:], ACT.Silu).then_inc(silu_ok, 1)

            def weigh(s, b, early=False):
                act.wait_ge(y_mm, s + 1)
                if not early:
                    act.wait_ge(scattered, 16 * (s - 1))
                nc.scalar.activation(Y[:, b, :], psY[b][:, 0:D], ACT.Copy, scale=slotw[:, bass.ds(s, 1)]).then_inc(Y_ok, 1)

            take_xt(0, 0, True)
            silu(0, 0, True)
            take_xt(1, 1, True)
            silu(1, 1, True)
            take_xt(2, 0)
            weigh(0, 0, True)
            silu(2, 0)
            take_xt(3, 1)
            weigh(1, 1, True)
            with act.Fori(0, (NS - 5) // 2) as i:
                for b in (1, 0):
                    s = 2 * i + 4 - b
                    silu(s, b)
                    take_xt(s + 1, 1 - b)
                    weigh(s - 1, 1 - b)
            silu(NS - 2, 1)
            take_xt(NS - 1, 0)
            weigh(NS - 3, 0)
            silu(NS - 1, 0)
            weigh(NS - 2, 1)
            weigh(NS - 1, 0)

        @block.vector
        def _(dve):
            dve.wait_ge(kv_in, 16)
            for b in range(B):
                nc.vector.bn_stats(kst[:, b, :], kv[:, b, :]).then_inc(k_stats, 1)
            dve.wait_ge(k_stats, B)
            for b in range(B):
                nc.vector.bn_aggr(kmv[:, b, :], kst[:, b, :]).then_inc(k_mean, 1)
            dve.wait_ge(k_mean, B)
            for b in range(B):
                nc.vector.tensor_scalar(kc[:, b, :], kv[:, b, :], kmv[:, b, 0:1], None, ALU.subtract).then_inc(k_cent, 1)

            def norm_stats(n, g, src, s0):
                if g > 0:
                    dve.wait_ge(mv_ok[n], G * g)
                for j in range(G):
                    nc.vector.bn_stats(st[:, n, j, :], src[:, s0 + j, :]).then_inc(stats_d[n], 1)
                dve.wait_ge(stats_d[n], G * g + G)
                if g > 0:
                    dve.wait_ge(ve_ok[n], g)
                for j in range(G):
                    nc.vector.bn_aggr(mv[:, n, j, :], st[:, n, j, :]).then_inc(mv_ok[n], 1)

            def maxima(g):
                ts, b = slice(G * g, G * g + G), g // (NG // B)
                dve.wait_ge(score_mm, g + 1)
                sc = psS[:, :].rearrange("p (t u) -> p t u", t=G)[:, :, b * U:(b + 1) * U]
                nc.vector.reduce_max(mx[:, ts], sc, AX.X).then_inc(mx_ok, 1)
                dve.wait_ge(mx_ok, g + 1)
                dve.wait_ge(r16_ok, g + 1)
                nc.vector.scalar_tensor_tensor(out=nb[:, ts], in0=mx[:, ts], scalar=-1.0, in1=r16[:, ts],
                                               op0=ALU.mult, op1=ALU.mult).then_inc(nb_ok, 1)

            def attended(g):
                ts = slice(G * g, G * g + G)
                dve.wait_ge(exp_ok, G * g + G)
                nc.vector.reciprocal(rz[:, ts], zsum[:, ts]).then_inc(rz_ok, 1)
                dve.wait_ge(rz_ok, g + 1)
                dve.wait_ge(q_ok, G * g + G)
                if g >= 2:
                    dve.wait_ge(u_ok, G * (g - 1))
                for j in range(G):
                    t, r = G * g + j, G * (g % 2) + j
                    if j % 2 == 0:
                        dve.wait_ge(pv_mm, 2 * g + j // 2 + 1)
                    nc.vector.scalar_tensor_tensor(out=zn[:, r, :], in0=psO[j // 2][:, (j % 2) * D:(j % 2 + 1) * D],
                                                   scalar=rz[:, t:t + 1], in1=qu[:, t, :],
                                                   op0=ALU.mult, op1=ALU.add).then_inc(z_ok, 1)
                dve.wait_ge(z_ok, G * g + G)
                norm_stats(1, g, zn, G * (g % 2))

            def ffn_sum(g):
                for j in range(G):
                    t, r = G * g + j, G * (g % 2) + j
                    dve.wait_ge(ng_ok, t + 1)
                    if j % 2 == 0:
                        dve.wait_ge(f_mm, 2 * g + j // 2 + 1)
                    nc.vector.tensor_tensor(qu[:, t, :], psO[j // 2][:, (j % 2) * D:(j % 2 + 1) * D], zn[:, r, :],
                                            ALU.add).then_inc(u_ok, 1)
                dve.wait_ge(u_ok, G * g + G)
                norm_stats(2, g, qu, G * g)

            def after_attention(g):
                dve.wait_ge(rstd_ok[2], g + 1)
                for t in range(G * g, G * g + G):
                    nc.vector.scalar_tensor_tensor(out=qu[:, t, :], in0=qu[:, t, :], scalar=ve[:, 2, t, 0:1],
                                                   in1=gammaB[:], op0=ALU.subtract, op1=ALU.mult).then_inc(v_ok, 1)
                dve.wait_ge(v_ok, G * g + G)
                dve.wait_ge(xb_ok, G * g + G)
                for t in range(G * g, G * g + G):
                    nc.vector.scalar_tensor_tensor(out=xs[:, t, :], in0=qu[:, t, :], scalar=rstd[:, 2, t:t + 1],
                                                   in1=xs[:, t, :], op0=ALU.mult, op1=ALU.add).then_inc(x1_ok, 1)
                dve.wait_ge(x1_ok, G * g + G)
                norm_stats(3, g, xs, G * g)

            def take_logits(g):
                dve.wait_ge(lg_mm, g + 1)
                nc.vector.tensor_copy(lg[:, G * g:G * g + G, :],
                                      psH[1][:, :].rearrange("p (t n) -> p t n", t=G)[:, :, 0:E]).then_inc(lg_ok, 1)

            for g in range(NG):
                dve.wait_ge(x_in[g], 16)
                norm_stats(0, g, xs, G * g)
                if g == 0:
                    maxima(0)
            dve.wait_ge(aw_in, 32)
            dve.wait_ge(vec_in, 48)
            for k in range(KD):
                nc.vector.tensor_scalar(aw1g[:, k, :], aw1[:, k, :], cols[:, 0, k:k + 1], None, ALU.mult).then_inc(w1g_ok, 1)
            nc.vector.tensor_tensor(bb[:, 0, :], rows[0:1, 0, :], rows[0:1, 1, :], ALU.add).then_inc(bb_d, 1)
            for a in range(3):
                dve.wait_ge(bb_d, 2 * a + 1)
                nc.vector.tensor_copy(bbp[:, a, :], bb[:, a, :]).then_inc(bb_ok if a == 2 else bb_d, 1)
                if a < 2:
                    dve.wait_ge(bb_d, 2 * a + 2)
                    nc.vector.tensor_tensor(bb[:, a + 1, :], bb[:, a, :], bbp[:, a, :], ALU.subtract).then_inc(bb_d, 1)
            dve.wait_ge(b1_mm, 1)
            nc.vector.tensor_tensor(b1f[:], psH[0][:, 0:KD], cols[:, 2, :], ALU.add).then_inc(b1_ok, 1)
            for i in range(NG + 3):
                if i >= 3:
                    take_logits(i - 3)
                if i < NG:
                    attended(i)
                if 1 <= i <= NG:
                    ffn_sum(i - 1)
                if i + 1 < NG:
                    maxima(i + 1)
                if 1 <= i <= NG:
                    after_attention(i - 1)

            n = [0]

            def link(ins):
                n[0] += 1
                ins.then_inc(step, 1)
                dve.wait_ge(step, n[0])

            v = nc.vector
            TE = (P, T, E)
            dve.wait_ge(const_ok, 2)
            dve.wait_ge(lg_ok, NG)
            dve.wait_ge(flat_out[NG - 2], 16)
            dve.wait_ge(flat_out[NG - 1], 16)
            dve.wait_ge(fT_tr, NG)
            prioB = bc(prio[:, None, :], TE)
            for c in range(TOPK):
                src = (lg, lg2)[c]
                link(v.reduce_max(m12[:, c, :], src[:], AX.X))
                link(v.tensor_tensor(pick[:], src[:], bc(m12[:, c, :, None], TE), ALU.is_ge))
                link(v.tensor_tensor(pick[:], pick[:], prioB, ALU.mult))
                link(v.reduce_max(pmax[:, c, :], pick[:], AX.X))
                link(v.tensor_tensor(oh[:, c, :, :], bc(pmax[:, c, :, None], TE), prioB, ALU.is_equal))
                if c == 0:
                    link(v.scalar_tensor_tensor(out=lg2[:], in0=oh[:, 0, :, :], scalar=-3e38, in1=lg[:],
                                                op0=ALU.mult, op1=ALU.add))
            v.tensor_tensor(dm[:], m12[:, 1, :], m12[:, 0, :], ALU.subtract).then_inc(dm_ok, 1)
            v.tensor_tensor(both[:].rearrange("p (t e) -> p t e", t=T), oh[:, 0, :, :], oh[:, 1, :, :], ALU.add).then_inc(both_ok, 1)
            dve.wait_ge(ex_ok, 1)
            link(v.tensor_scalar(den[:], ex[:], 1.0, None, ALU.add))
            link(v.reciprocal(wts[:, 0, :], den[:]))
            link(v.tensor_tensor(wts[:, 1, :], ex[:], wts[:, 0, :], ALU.mult))
            dve.wait_ge(count_mm, 1)
            link(v.tensor_copy(totE[:], psC[:, T * E:2 * T * E].rearrange("p (t e) -> p e t", t=T)))
            link(v.tensor_tensor_scan(incl[:].rearrange("p e t -> p (e t)"), first0[:].rearrange("p e t -> p (e t)"),
                                      totE[:].rearrange("p e t -> p (e t)"), 0.0, ALU.mult, ALU.add))
            v.tensor_scalar(tp[:], incl[:, :, T - 1], float(P - 1), None, ALU.add).then_inc(step, 1)
            n[0] += 1
            link(v.tensor_tensor(excl[:], incl[:], totE[:], ALU.subtract))
            link(v.tensor_scalar(nti[:], tp[:], P.bit_length() - 1, None, ALU.logical_shift_right))
            link(v.tensor_copy(ntf[:], nti[:]))
            link(v.tensor_tensor_scan(ends[:], ones8[:], ntf[:], 0.0, ALU.mult, ALU.add))
            link(v.tensor_tensor(starts[:], ends[:], ntf[:], ALU.subtract))
            link(v.scalar_tensor_tensor(out=base[:], in0=bc(starts[:, None, :], TE), scalar=float(P),
                                        in1=excl[:].rearrange("p e t -> p t e"), op0=ALU.mult, op1=ALU.add))
            link(v.tensor_tensor(rank[:], psC[:, 0:T * E].rearrange("p (t e) -> p t e", t=T), base[:], ALU.add))
            link(v.tensor_tensor(rsel[:], oh[:], bc(rank[:, None, :, :], (P, TOPK, T, E)), ALU.mult))
            link(v.reduce_sum(pos[:].rearrange("p (c t) -> p c t", c=TOPK), rsel[:], AX.X))
            link(v.tensor_copy(posi[:], pos[:]))
            v.tensor_scalar(hii[:], posi[:], P.bit_length() - 1, None, ALU.logical_shift_right).then_inc(step, 1)
            n[0] += 1
            link(v.tensor_scalar(loi[:], posi[:], P - 1, None, ALU.bitwise_and))
            v.tensor_copy(hif[:], hii[:]).then_inc(step, 1)
            n[0] += 1
            link(v.tensor_copy(lof[:], loi[:]))
            QS = (P, Q32, NS)
            v.tensor_tensor(slots[:, :, 2, :], bc(iota_s[:, None, :], QS), bc(hif[:, :, None], QS), ALU.is_equal).then_inc(ohhi_ok, 1)
            dve.wait_ge(ohhi_ok, 1)
            v.tensor_tensor(slots[:, :, 0, :], slots[:, :, 2, :], bc(pairv[:, :, None], QS), ALU.mult).then_inc(slots_ok, 1)
            for q in range(Q32):
                v.tensor_scalar(ohlo[:, q, :], iota_p[:], lof[:, q:q + 1], None, ALU.is_equal).then_inc(ohlo_ok, 1)
            link(v.tensor_tensor(ge[:], bc(iota_s[0:1, :, None], (1, NS, E)), bc(ends[0:1, None, :], (1, NS, E)), ALU.is_ge))
            link(v.reduce_sum(eidf[:], ge[:], AX.X))
            link(v.tensor_scalar(eid[:], eidf[:], float(E - 1), None, ALU.min))
            dve.wait_ge(slot_mm, 1)
            sval = psR[:, 0:NS]
            v.tensor_copy(slotw[:], psR[:, NS:2 * NS]).then_inc(step, 1)
            v.tensor_scalar(sk[:], sval, N + 0.5, -float(N), ALU.is_gt, ALU.mult).then_inc(step, 1)
            v.tensor_scalar(padg[:], sval, 0.5, pcol[:, 0:1], ALU.is_lt, ALU.mult).then_inc(step, 1)
            n[0] += 3
            link(v.tensor_scalar(pads[:], sval, 0.5, pcol[:, 1:2], ALU.is_lt, ALU.mult))
            link(v.tensor_tensor(stok[:], sk[:], sval, ALU.add))
            v.scalar_tensor_tensor(out=gi[:], in0=padg[:], scalar=-1.0, in1=stok[:], op0=ALU.add, op1=ALU.add).then_inc(step, 1)
            n[0] += 1
            link(v.scalar_tensor_tensor(out=si[:], in0=pads[:], scalar=-1.0, in1=stok[:], op0=ALU.add, op1=ALU.add))
            v.engine_nop().then_inc(route_ok, 1)

            def product(s, b, early=False):
                dve.wait_ge(val_mm, s + 1)
                dve.wait_ge(silu_ok, s + 1)
                if not early:
                    dve.wait_ge(A_tr, s - 1)
                v.tensor_tensor(A[:, b, :], psV[b][:], S[:, b, :], ALU.mult).then_inc(A_ok, 1)

            def take_at(s, first=False):
                dve.wait_ge(A_tr, s + 1)
                if not first:
                    dve.wait_ge(y_mm, s)
                v.tensor_copy(AT[:], psA[:].rearrange("p (k n) -> p k n", k=KF)).then_inc(AT_ok, 1)

            product(0, 0, True)
            take_at(0, True)
            product(1, 1, True)
            take_at(1)
            product(2, 0)
            with dve.Fori(0, (NS - 3) // 2) as i:
                for b in (1, 0):
                    s = 2 * i + 4 - b
                    take_at(s - 1)
                    product(s, b)
            take_at(NS - 1)

        @block.tensor
        def _(pe):
            pe.wait_ge(ident_ok, 1)
            pe.wait_ge(k_cent, B)
            for k in range(KD):
                for b in range(B):
                    c = (k * B + b) * U
                    last = nc.tensor.transpose(psT[0][:, c:c + U], kc[:, b, k * P:(k + 1) * P], ident[0:U, 0:U])
            last.then_inc(kT_tr, 1)

            def scores(g):
                pe.wait_ge(xT_in[g], 16)
                if g == 0:
                    pe.wait_ge(kT_ok, 1)
                else:
                    pe.wait_ge(exp_ok, G * g)
                for j in range(G):
                    t = G * g + j
                    for k in range(KD):
                        last = nc.tensor.matmul(psS[:, j * B * U:(j + 1) * B * U], xTs[:, k, t * P:(t + 1) * P], kT[:, k, :],
                                                start=(k == 0), stop=(k == KD - 1))
                last.then_inc(score_mm, 1)

            def prob_t(g):
                pe.wait_ge(exp_ok, G * g + G)
                if g > 0:
                    pe.wait_ge(pT_ok, g)
                for j in range(G):
                    last = nc.tensor.transpose(psPT[0:U, j * P:(j + 1) * P], prob[:, j, :], ident[:])
                last.then_inc(pT_tr, 1)

            def pv(g):
                pe.wait_ge(pT_ok, g + 1)
                for j in range(G):
                    if j % 2 == 0:
                        if g == 1:
                            pe.wait_ge(z_ok, j + 2)
                        elif g > 1:
                            pe.wait_ge(u_ok, G * (g - 2) + j + 2)
                    last = nc.tensor.matmul(psO[j // 2][:, (j % 2) * D:(j % 2 + 1) * D], probT[:, j * P:(j + 1) * P],
                                            kv[:, g // (NG // B), :], start=True, stop=True)
                    if j % 2 == 1:
                        last.then_inc(pv_mm, 1)

            def rows_t(g, tr):
                for k in range(KD):
                    for j in range(G):
                        last = nc.tensor.transpose(psT[k][:, j * P:(j + 1) * P], nf[:, G * (g % 2) + j, k * P:(k + 1) * P],
                                                   ident[:])
                last.then_inc(tr, 1)

            def attention_t(g):
                pe.wait_ge(n_ok, G * g + G)
                if g == 1:
                    pe.wait_ge(nT_ok, KD)
                elif g > 1:
                    pe.wait_ge(fT_ok, KD * (g - 1))
                rows_t(g, nT_tr)

            def ffn_up(g):
                pe.wait_ge(nT_ok, KD * (g + 1))
                if g == 0:
                    pe.wait_ge(w1g_ok, KD)
                    pe.wait_ge(b1_ok, 1)
                for m in range(KD):
                    if g > 0:
                        pe.wait_ge(h_ok, KD * (g - 1) + m + 1)
                    if m == 1 and g >= 2:
                        pe.wait_ge(lg_ok, g - 1)
                    for k in range(KD):
                        last = nc.tensor.matmul(psH[m][:], aw1g[:, k, m * P:(m + 1) * P], nT[:, k, :],
                                                start=(k == 0), stop=(k == KD - 1))
                    last.then_inc(h_mm, 1)

            def ffn_down(g):
                pe.wait_ge(h_ok, KD * (g + 1))
                if g == 0:
                    pe.wait_ge(bb3_in, 48)
                    pe.wait_ge(ones3_ok, 1)
                for j in range(G):
                    if j % 2 == 0:
                        if g + 1 < NG:
                            pe.wait_ge(z_ok, G * (g + 1) + j + 2)
                        else:
                            pe.wait_ge(u_ok, G * (g - 1) + j + 2)
                    o = psO[j // 2][:, (j % 2) * D:(j % 2 + 1) * D]
                    for k in range(KD):
                        nc.tensor.matmul(o, hT[:, k, j * P:(j + 1) * P], aw2[:, k, :], start=(k == 0), stop=False)
                    last = nc.tensor.matmul(o, ones3[:], bb3[:], start=False, stop=True)
                    if j % 2 == 1:
                        last.then_inc(f_mm, 1)

            def expert_t(g):
                pe.wait_ge(flat_ok, G * g + G)
                if g + 1 < NG:
                    pe.wait_ge(nT_ok, KD * (g + 2))
                else:
                    pe.wait_ge(fT_ok, KD * (NG - 1))
                rows_t(g, fT_tr)

            def logits(g):
                pe.wait_ge(fT_ok, KD * (g + 1))
                if g == 0:
                    pe.wait_ge(wr_in, 16)
                if g + 1 < NG:
                    pe.wait_ge(h_ok, KD * (g + 2))
                else:
                    pe.wait_ge(lg_ok, NG - 1)
                for j in range(G):
                    for k in range(KD):
                        last = nc.tensor.matmul(psH[1][:, j * P:(j + 1) * P], nT[:, k, j * P:(j + 1) * P], wr[:, k, :],
                                                start=(k == 0), stop=(k == KD - 1))
                last.then_inc(lg_mm, 1)

            scores(0)
            pe.wait_ge(aw_in, 32)
            pe.wait_ge(vec_in, 48)
            for m in range(KD):
                for k in range(KD):
                    last = nc.tensor.matmul(psH[0][:, m:m + 1], aw1[:, k, m * P:(m + 1) * P], cols[:, 1, k:k + 1],
                                            start=(k == 0), stop=(k == KD - 1))
            last.then_inc(b1_mm, 1)
            for i in range(NG + 2):
                if 1 <= i <= NG:
                    attention_t(i - 1)
                if i < NG:
                    prob_t(i)
                if 1 <= i <= NG:
                    ffn_up(i - 1)
                if i < NG:
                    pv(i)
                if 1 <= i <= NG:
                    ffn_down(i - 1)
                if i >= 2:
                    expert_t(i - 2)
                if i + 1 < NG:
                    scores(i + 1)
                if i >= 2:
                    logits(i - 2)

            pe.wait_ge(both_ok, 1)
            nc.tensor.matmul(psC[:, 0:T * E], tri[:], both[:], start=True, stop=True)
            nc.tensor.matmul(psC[:, T * E:2 * T * E], onesb[:], both[:], start=True, stop=True).then_inc(count_mm, 1)
            pe.wait_ge(slots_ok, 1)
            pe.wait_ge(slotsw_ok, 1)
            for q in range(Q32):
                pe.wait_ge(ohlo_ok, q + 1)
                last = nc.tensor.matmul(psR[:, 0:3 * NS], ohlo[:, q, :], slots[:, q, :, :].rearrange("p a s -> p (a s)"),
                                        start=(q == 0), stop=(q == Q32 - 1))
            last.then_inc(slot_mm, 1)

            pe.wait_ge(route_ok, 1)
            pe.wait_ge(ew_in, 32 * E)

            def expert(s):
                return pe.value_load(eid[0:1, bass.ds(s, 1)], min_val=0, max_val=E - 1)

            def w1_at(e, k, h):
                return W1[:, bass.ds(e, 1), k, h * F:(h + 1) * F].rearrange("p a f -> p (a f)")

            def rows_in(s, x, n, first=False):
                pe.wait_ge(gathered[x], 16 * n)
                if not first:
                    pe.wait_ge(XT_ok, s)
                for k in range(KD):
                    last = nc.tensor.transpose(psX[:, k * P:(k + 1) * P], X[:, x, k * P:(k + 1) * P], ident[:])
                last.then_inc(X_tr, 1)

            def gate(s, b, e, early=False):
                pe.wait_ge(XT_ok, s + 1)
                if not early:
                    pe.wait_ge(silu_ok, s - 1)
                for k in range(KD):
                    last = nc.tensor.matmul(psG[b][:], XT[:, b, k, :], w1_at(e, k, 1), start=(k == 0), stop=(k == KD - 1))
                last.then_inc(gate_mm, 1)

            def val(s, b, e, early=False):
                if not early:
                    pe.wait_ge(A_ok, s - 1)
                for k in range(KD):
                    last = nc.tensor.matmul(psV[b][:], XT[:, b, k, :], w1_at(e, k, 0), start=(k == 0), stop=(k == KD - 1))
                last.then_inc(val_mm, 1)

            def act_t(s, b, first=False):
                pe.wait_ge(A_ok, s + 1)
                if not first:
                    pe.wait_ge(AT_ok, s)
                for k in range(KF):
                    last = nc.tensor.transpose(psA[:, k * P:(k + 1) * P], A[:, b, k * P:(k + 1) * P], ident[:])
                last.then_inc(A_tr, 1)

            def down(s, b, e, early=False):
                pe.wait_ge(AT_ok, s + 1)
                if not early:
                    pe.wait_ge(Y_ok, s - 1)
                for k in range(KF):
                    last = nc.tensor.matmul(psY[b][:, 0:D], AT[:, k, :],
                                            W2[:, bass.ds(e, 1), k, :].rearrange("p a c -> p (a c)"),
                                            start=(k == 0), stop=(k == KF - 1))
                last.then_inc(y_mm, 1)

            def steady(s, b, x, n):
                e = expert(s)
                gate(s, b, e)
                act_t(s - 1, 1 - b)
                val(s, b, e)
                if n is not None:
                    rows_in(s + 1, x, n)
                down(s - 1, 1 - b, expert(s - 1))

            rows_in(0, 0, 1, True)
            e = expert(0)
            gate(0, 0, e, True)
            val(0, 0, e, True)
            rows_in(1, 1, 1)
            e = expert(1)
            gate(1, 1, e, True)
            act_t(0, 0, True)
            val(1, 1, e, True)
            rows_in(2, 2, 1)
            down(0, 0, expert(0), True)
            e = expert(2)
            gate(2, 0, e)
            act_t(1, 1)
            val(2, 0, e)
            rows_in(3, 3, 1)
            down(1, 1, expert(1), True)
            with pe.Fori(0, (NS - 3) // NX - 1) as i:
                for j in range(NX):
                    steady(NX * i + 3 + j, (3 + j) % 2, j, i + 2)
            last_round = (NS - 3) // NX - 1
            for j in range(NX):
                steady(NX * last_round + 3 + j, (3 + j) % 2, j, last_round + 2 if j < NX - 1 else None)
            act_t(NS - 1, 0)
            down(NS - 1, 0, expert(NS - 1))


def kernel(x, ctx_1024, L0_xattn_W1, L0_xattn_b1, L0_xattn_W2, L0_xattn_b2, L0_xattn_gamma, L0_xattn_beta,
           L0_ffn_Wr, L0_ffn_W1, L0_ffn_W2):
    import numpy as np
    import concourse.bacc as bacc
    from concourse import mybir
    from concourse.bass_utils import run_bass_kernel_spmd

    x = np.asarray(x)
    Bb, R, D = x.shape
    N = Bb * R
    flat = np.ascontiguousarray(x.reshape(N, D))
    ins = {
        "x": flat,
        "xT": np.ascontiguousarray(flat.T),
        "ctx_kv": np.ascontiguousarray(ctx_1024),
        "aW1": np.ascontiguousarray(L0_xattn_W1),
        "aW2": np.ascontiguousarray(L0_xattn_W2),
        "vec_cols": np.ascontiguousarray(np.stack([L0_xattn_gamma, L0_xattn_beta, L0_xattn_b1])
                                         .reshape(3, D // 128, 128).transpose(2, 0, 1)),
        "b2": np.ascontiguousarray(L0_xattn_b2),
        "gamma": np.ascontiguousarray(L0_xattn_gamma),
        "beta": np.ascontiguousarray(L0_xattn_beta),
        "WrT": np.ascontiguousarray(np.asarray(L0_ffn_Wr).T),
        "eW1": np.ascontiguousarray(np.asarray(L0_ffn_W1).transpose(0, 2, 1)),
        "eW2": np.ascontiguousarray(np.asarray(L0_ffn_W2).transpose(0, 2, 1)),
    }
    nc = bacc.Bacc("TRN2", target_bir_lowering=False, num_devices=1)
    aps = [nc.dram_tensor(f"in_{k}", v.shape, mybir.dt.from_np(v.dtype), kind="ExternalInput").ap() for k, v in ins.items()]
    flat_dram = nc.dram_tensor("flat_rows", (N, D), mybir.dt.float32, kind="Internal").ap()
    out = nc.dram_tensor("out_rows", (N + 128, D), mybir.dt.float32, kind="ExternalOutput").ap()
    xattn_then_sparse_experts(nc, *aps, flat_dram, out)
    r = run_bass_kernel_spmd(nc, [{f"in_{k}": v for k, v in ins.items()}], core_ids=[0])
    return r.results[0]["out_rows"][:N].reshape(Bb, R, D)
```

```python
import concourse.bass as bass
from concourse import mybir
from contextlib import ExitStack


def xattn_then_sparse_experts(nc, x, xT, ctx_kv, aW1, aW2, vec_cols, b2, gamma, beta, WrT, eW1, eW2, flat_dram, out):
    f32, f32r, bf16, i32 = mybir.dt.float32, mybir.dt.float32r, mybir.dt.bfloat16, mybir.dt.int32
    ACT = mybir.ActivationFunctionType
    ALU = mybir.AluOpType
    AX = mybir.AxisListType

    P = 128
    N, D = x.shape
    B, U, _ = ctx_kv.shape
    E, _, F2 = eW1.shape
    F = F2 // 2
    KD = D // P
    KF = F // P
    T = N // P
    G = 4
    NG = T // G
    TH = T // B
    TOPK = 2
    Q32 = TOPK * T
    NS = TOPK * T + E - 1
    SCALE = 1.0 / 16.0
    EPS_IN, EPS_LN = 1e-5, 1e-6
    assert D == 256 and NS % 4 == 3

    x_v = x.rearrange("(t p) c -> p t c", p=P)
    xT_v = xT.rearrange("(k p) n -> p k n", p=P)
    out_v = out[0:N, :].rearrange("(t p) c -> p t c", p=P)
    flat_v = flat_dram.rearrange("(t p) c -> p t c", p=P)
    w1_v = eW1.rearrange("e (k p) f -> p e k f", p=P)
    w2_v = eW2.rearrange("e (k p) c -> p e k c", p=P)

    ctx = ExitStack()
    with ctx:
        def sb(name, shape, dt=f32):
            return ctx.enter_context(nc.sbuf_tensor(name, shape, dt))

        def sem(name):
            return ctx.enter_context(nc.semaphore(name))

        W1h = sb("expert_w1_high", [P, E, KD, F2], f32r)
        W2h = sb("expert_w2_high", [P, E, KF, D], f32r)
        late = sb("late", [P, (E * KD * F2 + E * KF * D) // 2])
        W1l = late[:, 0:E * KD * F2 // 2].bitcast(bf16).rearrange("p (e k f) -> p e k f", e=E, k=KD)
        W2l = late[:, E * KD * F2 // 2:].bitcast(bf16).rearrange("p (e k c) -> p e k c", e=E, k=KF)
        xs = late[:, 2 * T * D:3 * T * D].rearrange("p (t c) -> p t c", t=T)
        qu = late[:, T * D:2 * T * D].rearrange("p (t c) -> p t c", t=T)
        zn = sb("zn", [P, 2 * G, D])
        work = sb("work", [P, 2 * KD * G * P + 2 * G * D])
        nT = work[:, 0:KD * G * P].rearrange("p (k n) -> p k n", k=KD)
        hT = work[:, KD * G * P:2 * KD * G * P].rearrange("p (k n) -> p k n", k=KD)
        nf = work[:, 2 * KD * G * P:].rearrange("p (t c) -> p t c", c=D)
        xt_area = sb("xt_area", [P, 2 * KD * G * P])
        xTs = xt_area[:, :].rearrange("p (g k n) -> p g k n", g=2, k=KD)
        prob = sb("prob", [P, G, U])
        probT = sb("probT", [U, G * P])
        kv = sb("kv", [U, B, D])
        kc = work[0:U, 0:B * D].rearrange("p (b c) -> p b c", b=B)
        rows = work[0:1, 2 * D:4 * D].rearrange("p (a c) -> p a c", a=2)
        bb = work[0:1, 4 * D:7 * D].rearrange("p (a c) -> p a c", a=3)
        bbp = work[0:1, 7 * D:9 * D - D // 2].bitcast(bf16).rearrange("p (a c) -> p a c", a=3)
        kT = sb("kT", [P, KD, B * U])
        aw1 = sb("aw1", [P, KD, D])
        aw1g = sb("aw1g", [P, KD, D])
        aw2 = sb("aw2", [P, KD, D])
        wr = sb("wr", [P, KD, P])
        cols = sb("cols", [P, 3, KD])
        b1f = sb("b1f", [P, KD])
        bb3 = sb("bb3", [3, D], bf16)
        ones3 = sb("ones3", [3, P], bf16)
        gammaB = sb("gammaB", [P, D])
        betaB = sb("betaB", [P, D])
        ident = sb("ident", [P, P])
        zero = sb("zero", [P, D])
        epsr = sb("epsr", [P, 2, G, 2])
        mhalf = sb("mhalf", [P, G])
        cscale = sb("cscale", [P, G])
        cneg = sb("cneg", [P, G])
        kst = sb("kst", [U, B, 6])
        kmv = sb("kmv", [U, B, 2])
        st = sb("st", [P, 4, G, 6])
        mv = sb("mv", [P, 4, G, 2])
        ve = sb("ve", [P, 4, T, 2])
        rstd = sb("rstd", [P, 4, T])
        mr = sb("mr", [P, 4, T])
        nmr = sb("nmr", [P, 4, T])
        r16 = sb("r16", [P, T])
        mx = sb("mx", [P, T])
        nb = sb("nb", [P, T])
        zsum = sb("zsum", [P, T])
        rz = sb("rz", [P, T])
        wts = sb("wts", [P, TOPK, T])
        prio = sb("prio", [P, E])
        tri = sb("tri", [P, P], bf16)
        onesb = sb("onesb", [P, P], bf16)
        first0 = sb("first0", [P, E, T])
        ones8 = sb("ones8", [P, E])
        iota_s = sb("iota_s", [P, NS])
        iota_p = sb("iota_p", [P, P], bf16)
        qp1 = sb("qp1", [P, Q32], bf16)
        pcol = sb("pcol", [P, 3])
        eid = sb("eid", [1, NS], i32)
        slotw = sb("slotw", [P, NS])
        gi = sb("gi", [P, NS], i32)
        si = sb("si", [P, NS], i32)
        both = sb("both", [P, T * E], bf16)

        NX = 4
        free = [0]
        zn_flat = zn[:, :, :].rearrange("p t c -> p (t c)")

        def scratch(*dims):
            size = 1
            for d in dims:
                size *= d
            ap = zn_flat[:, free[0]:free[0] + size]
            free[0] += size
            names = "abc"[:len(dims)]
            if len(dims) == 1:
                return ap
            return ap.rearrange(f"p ({' '.join(names)}) -> p {' '.join(names)}", **dict(zip(names, dims)))

        lg = sb("lg", [P, T, E])
        old_w1 = aw1[:, :, :].rearrange("p k n -> p (k n)")
        lg2 = old_w1[:, 0:T * E].rearrange("p (t e) -> p t e", t=T)
        pick = old_w1[:, T * E:2 * T * E].rearrange("p (t e) -> p t e", t=T)
        rsel = old_w1[:, 2 * T * E:4 * T * E].rearrange("p (c t e) -> p c t e", c=TOPK, t=T)
        oh = scratch(TOPK, T * E).rearrange("p c (t e) -> p c t e", t=T)
        totE, incl, excl = scratch(E, T), scratch(E, T), scratch(E, T)
        base, rank = scratch(T, E), scratch(T, E)
        m12, pmax = scratch(TOPK, T), scratch(TOPK, T)
        dm, ex, den = scratch(T), scratch(T), scratch(T)
        free[0] = NX * D
        ntf, ends, starts = scratch(E), scratch(E), scratch(E)
        tp, nti = scratch(E).bitcast(i32), scratch(E).bitcast(i32)
        posi, hii, loi = (scratch(Q32).bitcast(i32) for _ in range(3))
        pos, lof = scratch(Q32), scratch(Q32)
        ROUND_DOWN = 2 ** 15 - P
        hib = scratch(Q32 // 2).bitcast(bf16)
        wrest = scratch(2, Q32)
        wpart = scratch(3, Q32 // 2).bitcast(bf16)
        old_prob = prob[:, :, :].rearrange("p t u -> p (t u)")
        sval, sk, stok, padg, pads, w01 = (old_prob[:, a * NS:(a + 1) * NS] for a in range(6))
        iota_sq = scratch(NS * Q32 // 2).bitcast(bf16).rearrange("p (s q) -> p s q", s=NS)
        ge = probT[0:1, 0:NS * E].rearrange("p (s e) -> p s e", e=E)
        eidf = probT[0:1, NS * E:NS * E + NS]
        assert free[0] <= 2 * G * D and NS * (E + 1) <= G * P
        ohlo = xt_area[:, :].bitcast(bf16).rearrange("p (q n) -> p q n", q=Q32)
        work_b = work[:, 0:6 * NS * Q32 // 2].bitcast(bf16).rearrange("p (a s q) -> p a s q", a=6, s=NS)
        ohs, whose, weight = work_b[:, 0], work_b[:, 1:3], work_b[:, 3:6]

        at = [NS * Q32 // 2, 0]

        def area(i, n):
            at[i] += n
            return (work, xt_area)[i][:, at[i] - n:at[i]]

        X = zn_flat[:, 0:NX * D].rearrange("p (b c) -> p b c", b=NX)
        S = area(0, 2 * F).rearrange("p (b f) -> p b f", b=2)
        A = area(0, 2 * F).rearrange("p (b f) -> p b f", b=2)
        XTb = work[:, 3 * NS * Q32:3 * NS * Q32 + D].bitcast(bf16).rearrange("p (b k n) -> p b k n", b=2, k=KD)
        Y = area(1, 2 * D).rearrange("p (b c) -> p b c", b=2)
        ATb = area(1, F // 2).bitcast(bf16).rearrange("p (k n) -> p k n", k=KF)

        chunks, frees = [], []

        def w1_chunks(e, free_at):
            for k in range(KD):
                chunks.append((w1_v[:, e, k, :], W1h[:, e, k, :], W1l[:, e, k, :]))
                frees.append(free_at)

        def w2_chunk(e, free_at):
            chunks.append((w2_v[:, e, :, :], W2h[:, e, :, :].rearrange("p k c -> p (k c)"),
                           W2l[:, e, :, :].rearrange("p k c -> p (k c)")))
            frees.append(free_at)

        for e in range(E // 2):
            w1_chunks(e, None)
        for g in range(NG):
            w1_chunks(E // 2 + g, ("qu", g))
            if g > 0:
                w2_chunk(2 * g - 2, ("xs", g - 1))
                w2_chunk(2 * g - 1, ("xs", g - 1))
        w2_chunk(E - 2, ("xs", NG - 1))
        w2_chunk(E - 1, ("xs", NG - 1))
        NC = len(chunks)
        DVE_SPLIT = (((), ()),) * NG + (((), (8, 10)), ((), (12, 14, 15, 16)))
        DVE_CHUNKS = tuple(c for two in DVE_SPLIT for one in two for c in one)
        spare = xt_area[:, :].rearrange("p (b f) -> p b f", b=2)
        MORE = 7
        place = [c % 2 if c < MORE else (2, 3, 1, 0)[(c - MORE) % 4] for c in range(NC)]
        LOAD = (((2,), ()), ((3, 4), ()), ((), (5, 6)), ((7, 8), (9, 10)), ((11, 12), (13, 14)), ((15, 16, 17, 18, 19, 20), ()))
        ROUND = (((), ()), ((1, 2), ()), ((3, 4), ()), ((5, 6), (7,)), ((8, 9, 10), (11, 12)), ((13, 14), ()))
        ROUND_LATE = (15,)
        SPLIT = (((), (1, 2)), ((), ()), ((), (3, 4)), ((), (5, 6)), ((), (7, 9)), ((11,), (13,)))

        def rest(table):
            return range(max(c for two in table for one in two for c in one) + 1, NC)

        def staged(c):
            return stage[:, place[c], :] if place[c] < 2 else spare[:, place[c] - 2, :]

        def uses(c):
            return place[:c + 1].count(place[c])

        def before(c):
            return max((d for d in range(c) if place[d] == place[c]), default=None)

        def split_count(c):
            return sum((d in DVE_CHUNKS) == (c in DVE_CHUNKS) for d in range(c + 1))

        with nc.sbuf_tensor("stage", [P, 2, F2], f32) as stage:
            pass
        XTh, XTl = (sb(name, [P, 2, KD, P], f32r) for name in ("XT_high", "XT_low"))
        ATh, ATl = (sb(name, [P, KF, P], f32r) for name in ("AT_high", "AT_low"))

        bank = [ctx.enter_context(nc.psum_tensor(f"bank{i}", [P, 512], f32)) for i in range(8)]
        psH = [bank[0], bank[1]]
        psS, psPT = bank[2], bank[3]
        psO = [bank[4], bank[5]]
        psT = [bank[6], bank[7]]
        psG, psV, psY = [bank[0], bank[1]], [bank[2], bank[3]], [bank[4], bank[5]]
        psX, psA = bank[6], bank[7]
        psC, psR, psW = bank[2], bank[3], bank[5]

        kv_in, aw_in, vec_in, wr_in = sem("kv_in"), sem("aw_in"), sem("vec_in"), sem("wr_in")
        x_in = [sem(f"x_in{g}") for g in range(NG)]
        xT_in = [sem(f"xT_in{g}") for g in range(NG)]
        bc_in = sem("bc_in")
        stage_in = [sem(f"stage_in{b}") for b in range(4)]
        high_ok, low_pool, low_dve = sem("high_ok"), sem("low_pool"), sem("low_dve")
        bb3_in, spare_out = sem("bb3_in"), sem("spare_out")
        x1_out = [sem(f"x1_out{g}") for g in range(NG)]
        flat_out = [sem(f"flat_out{g}") for g in range(NG)]
        ident0, ident_ok, zero_ok, ones3_ok, wr0 = sem("ident0"), sem("ident_ok"), sem("zero_ok"), sem("ones3_ok"), sem("wr0")
        cst_tmp, const_ok = sem("cst_tmp"), sem("const_ok")
        k_stats, k_mean, k_cent, kT_tr, kT_ok = sem("k_stats"), sem("k_mean"), sem("k_cent"), sem("kT_tr"), sem("kT_ok")
        w1g_ok, b1_mm, b1_ok, bb_d, bb_ok = sem("w1g_ok"), sem("b1_mm"), sem("b1_ok"), sem("bb_d"), sem("bb_ok")
        stats_d = [sem(f"stats_d{n}") for n in range(4)]
        mv_ok = [sem(f"mv_ok{n}") for n in range(4)]
        ve_ok = [sem(f"ve_ok{n}") for n in range(4)]
        rstd_ok = [sem(f"rstd_ok{n}") for n in range(4)]
        mr_ok = [sem(f"mr_ok{n}") for n in range(4)]
        nmr_ok = [sem(f"nmr_ok{n}") for n in range(4)]
        r16_ok, q_ok = sem("r16_ok"), sem("q_ok")
        score_mm, mx_ok, nb_ok, exp_ok = sem("score_mm"), sem("mx_ok"), sem("nb_ok"), sem("exp_ok")
        pT_tr, pT_ok, pv_mm, rz_ok, z_ok = sem("pT_tr"), sem("pT_ok"), sem("pv_mm"), sem("rz_ok"), sem("z_ok")
        n_ok, nT_tr, nT_ok, h_mm, h_ok, f_mm = sem("n_ok"), sem("nT_tr"), sem("nT_ok"), sem("h_mm"), sem("h_ok"), sem("f_mm")
        ng_ok, u_ok, xb_ok, v_ok, x1_ok = sem("ng_ok"), sem("u_ok"), sem("xb_ok"), sem("v_ok"), sem("x1_ok")
        flat_ok, fT_tr, fT_ok, lg_mm, lg_ok = sem("flat_ok"), sem("fT_tr"), sem("fT_ok"), sem("lg_mm"), sem("lg_ok")
        step = sem("step")
        iota_sq_ok, ohs_ok, whose_ok = sem("iota_sq_ok"), sem("ohs_ok"), sem("whose_ok")
        wts_ok, wpart_ok, weight_pool, weight_dve = sem("wts_ok"), sem("wpart_ok"), sem("weight_pool"), sem("weight_dve")
        weight_mm, slotw_ok, gi_ok, eid_ok = sem("weight_mm"), sem("slotw_ok"), sem("gi_ok"), sem("eid_ok")
        dm_ok, ex_ok, both_ok, count_mm = sem("dm_ok"), sem("ex_ok"), sem("both_ok"), sem("count_mm")
        ohlo_ok, slot_mm, route_ok = sem("ohlo_ok"), sem("slot_mm"), sem("route_ok")
        gathered = [sem(f"gathered{b}") for b in range(NX)]
        scattered = sem("scattered")
        X_tr, XTh_ok, XTb_ok, XTl_ok = sem("X_tr"), sem("XTh_ok"), sem("XTb_ok"), sem("XTl_ok")
        gate_mm, val_mm = sem("gate_mm"), sem("val_mm")
        silu_ok, A_ok, A_tr, y_mm, Y_ok = sem("silu_ok"), sem("A_ok"), sem("A_tr"), sem("y_mm"), sem("Y_ok")
        ATh_ok, ATb_ok, ATl_ok = sem("ATh_ok"), sem("ATb_ok"), sem("ATl_ok")

        block = ctx.enter_context(nc.Block())

        def bc(ap, shape):
            return ap.broadcast_to(shape)

        def wait_split(eng, c):
            eng.wait_ge(low_dve if c in DVE_CHUNKS else low_pool, split_count(c))

        def wait_place(eng, c):
            if frees[c] is not None:
                what, g = frees[c]
                eng.wait_ge(x1_ok, G * g + G)
                if what == "xs":
                    eng.wait_ge(x1_out[g], 16)
                    eng.wait_ge(flat_ok, G * g + G)

        def split_low(eng, c):
            eng.wait_ge(high_ok, c + 1)
            wait_place(eng, c)
            low = chunks[c][2]
            eng.tensor_tensor(low, staged(c), chunks[c][1].bitcast(f32), ALU.subtract).then_inc(
                low_dve if c in DVE_CHUNKS else low_pool, 1)

        @block.sync
        def _(sp):
            sp.dma_start(kv[:], ctx_kv.rearrange("b u c -> u b c")).then_inc(kv_in, 16)
            def load_x(g):
                ts = slice(g * G, (g + 1) * G)
                sp.dma_start(xs[:, ts, :], x_v[:, ts, :]).then_inc(x_in[g], 16)

            def load_xT(g):
                if g >= 2:
                    sp.wait_ge(score_mm, g - 1)
                sp.dma_start(xTs[:, g % 2, :, :], xT_v[:, :, g * G * P:(g + 1) * G * P]).then_inc(xT_in[g], 16)

            def load_chunk(c):
                if before(c) is not None:
                    wait_split(sp, before(c))
                elif place[c] >= 2:
                    sp.wait_ge(score_mm, NG)
                src = chunks[c][0]
                dst = staged(c)
                if len(src.shape) == 3:
                    dst = dst.rearrange("p (k c) -> p k c", k=KF)
                sp.dma_start(dst, src).then_inc(stage_in[place[c]], 16)

            def store_x1(g):
                ts = slice(G * g, G * g + G)
                sp.wait_ge(x1_ok, G * g + G)
                sp.dma_start(out_v[:, ts, :], xs[:, ts, :]).then_inc(x1_out[g], 16)

            def store_flat(g):
                ts, rs = slice(G * g, G * g + G), slice(G * (g % 2), G * (g % 2) + G)
                sp.wait_ge(flat_ok, G * g + G)
                sp.dma_start(flat_v[:, ts, :], nf[:, rs, :]).then_inc(flat_out[g], 16)

            load_x(0)
            load_xT(0)
            sp.dma_start(cols[:], vec_cols).then_inc(vec_in, 16)
            sp.dma_start(rows[0:1, 0, :], b2[None, :]).then_inc(vec_in, 16)
            sp.dma_start(rows[0:1, 1, :], beta[None, :]).then_inc(vec_in, 16)
            sp.dma_start(aw1[:], aW1.rearrange("(k p) n -> p k n", p=P)).then_inc(aw_in, 16)
            load_x(1)
            load_xT(1)
            sp.dma_start(gammaB[:], bc(gamma[None, :], (P, D))).then_inc(bc_in, 16)
            sp.dma_start(betaB[:], bc(beta[None, :], (P, D))).then_inc(bc_in, 16)
            sp.dma_start(aw2[:], aW2.rearrange("(k p) n -> p k n", p=P)).then_inc(aw_in, 16)
            load_chunk(0)
            load_chunk(1)
            load_x(2)
            sp.wait_ge(wr0, 1)
            sp.dma_start(wr[:, :, 0:E], WrT.rearrange("(k p) e -> p k e", p=P)).then_inc(wr_in, 16)
            sp.wait_ge(zero_ok, 1)
            sp.dma_start(out[N:N + P, :], zero[:]).then_inc(spare_out, 16)
            sp.wait_ge(bb_ok, 1)
            for a in range(3):
                sp.dma_start(bb3[a:a + 1, :], bbp[0:1, a, :]).then_inc(bb3_in, 16)
            load_x(3)
            for i in range(NG + 2):
                if i + 2 < NG:
                    load_xT(i + 2)
                for c in LOAD[i][0]:
                    load_chunk(c)
                if i >= 2:
                    store_x1(i - 2)
                    store_flat(i - 2)
                for c in LOAD[i][1]:
                    load_chunk(c)
            for c in rest(LOAD):
                load_chunk(c)
            sp.wait_ge(spare_out, 16)
            for g in range(NG):
                sp.wait_ge(x1_out[g], 16)
                sp.wait_ge(flat_out[g], 16)

        @block.gpsimd
        def _(pool):
            nc.gpsimd.memset(ident[:], 0.0).then_inc(ident0, 1)
            nc.gpsimd.memset(wr[:], 0.0).then_inc(wr0, 1)
            pool.wait_ge(ident0, 1)
            nc.gpsimd.affine_select(out=ident[:], in_=ident[:], compare_op=ALU.not_equal, fill=1.0, base=0,
                                    pattern=[[-1, P]], channel_multiplier=1).then_inc(ident_ok, 1)
            nc.gpsimd.memset(mhalf[:], -0.5).then_inc(cst_tmp, 1)
            nc.gpsimd.memset(cscale[:], SCALE).then_inc(cst_tmp, 1)
            nc.gpsimd.memset(cneg[:], -1.0).then_inc(cst_tmp, 1)
            nc.gpsimd.memset(epsr[:], 0.0).then_inc(cst_tmp, 1)
            pool.wait_ge(cst_tmp, 4)
            nc.gpsimd.memset(epsr[:, 0, :, 1:2], EPS_IN).then_inc(cst_tmp, 1)
            nc.gpsimd.memset(epsr[:, 1, :, 1:2], EPS_LN).then_inc(cst_tmp, 1)
            pool.wait_ge(cst_tmp, 6)

            def norm(n, g):
                ts = slice(G * g, G * g + G)
                pool.wait_ge(mv_ok[n], G * g + G)
                nc.gpsimd.tensor_tensor(ve[:, n, ts, :], mv[:, n, :, :], epsr[:, 1 if n in (1, 2) else 0, :, :],
                                        ALU.add).then_inc(ve_ok[n], 1)
                pool.wait_ge(ve_ok[n], g + 1)
                nc.gpsimd.tensor_tensor(rstd[:, n, ts], ve[:, n, ts, 1], mhalf[:], ALU.pow).then_inc(rstd_ok[n], 1)
                if n == 2:
                    return
                pool.wait_ge(rstd_ok[n], g + 1)
                nc.gpsimd.tensor_tensor(mr[:, n, ts], ve[:, n, ts, 0], rstd[:, n, ts], ALU.mult).then_inc(mr_ok[n], 1)
                if n == 0:
                    nc.gpsimd.tensor_tensor(r16[:, ts], rstd[:, n, ts], cscale[:], ALU.mult).then_inc(r16_ok, 1)
                pool.wait_ge(mr_ok[n], g + 1)
                nc.gpsimd.tensor_tensor(nmr[:, n, ts], mr[:, n, ts], cneg[:], ALU.mult).then_inc(nmr_ok[n], 1)

            def gamma_n(g):
                for j in range(G):
                    r = G * (g % 2) + j
                    pool.wait_ge(n_ok, G * g + j + 1)
                    nc.gpsimd.tensor_tensor(zn[:, r, :], nf[:, r, :], gammaB[:], ALU.mult).then_inc(ng_ok, 1)

            def x_beta(g):
                pool.wait_ge(q_ok, G * g + G)
                for t in range(G * g, G * g + G):
                    nc.gpsimd.tensor_tensor(xs[:, t, :], xs[:, t, :], betaB[:], ALU.add).then_inc(xb_ok, 1)

            norm(0, 0)
            nc.gpsimd.memset(ones3[:], 1.0).then_inc(ones3_ok, 1)
            nc.gpsimd.memset(zero[:], 0.0).then_inc(zero_ok, 1)
            norm(0, 1)
            nc.gpsimd.memset(onesb[:], 1.0).then_inc(cst_tmp, 1)
            nc.gpsimd.memset(first0[:], 1.0).then_inc(cst_tmp, 1)
            nc.gpsimd.memset(ones8[:], 1.0).then_inc(cst_tmp, 1)
            nc.gpsimd.iota(iota_s[:], [[P, NS]], base=0, channel_multiplier=0,
                           allow_small_or_imprecise_dtypes=True).then_inc(cst_tmp, 1)
            nc.gpsimd.iota(iota_p[:], [[1, P]], base=0, channel_multiplier=0,
                           allow_small_or_imprecise_dtypes=True).then_inc(cst_tmp, 1)
            nc.gpsimd.iota(prio[:], [[-1, E]], base=E, channel_multiplier=0,
                           allow_small_or_imprecise_dtypes=True).then_inc(cst_tmp, 1)
            nc.gpsimd.iota(qp1[:], [[1, Q32]], base=1, channel_multiplier=0,
                           allow_small_or_imprecise_dtypes=True).then_inc(cst_tmp, 1)
            nc.gpsimd.iota(pcol[:, 0:2], [[N, 2]], base=P, channel_multiplier=1,
                           allow_small_or_imprecise_dtypes=True).then_inc(cst_tmp, 1)
            nc.gpsimd.iota(pcol[:, 2:3], [[1, 1]], base=0, channel_multiplier=1,
                           allow_small_or_imprecise_dtypes=True).then_inc(cst_tmp, 1)
            pool.wait_ge(cst_tmp, 15)
            nc.gpsimd.affine_select(out=tri[:], in_=onesb[:], compare_op=ALU.is_gt, fill=0.0, base=0,
                                    pattern=[[1, P]], channel_multiplier=-1).then_inc(const_ok, 1)
            nc.gpsimd.memset(first0[:, :, 0:1], 0.0).then_inc(const_ok, 1)
            split_low(nc.gpsimd, 0)
            pool.wait_ge(bc_in, 32)
            for i in range(NG + 2):
                if i >= 2:
                    norm(2, i - 2)
                if 1 <= i <= NG:
                    gamma_n(i - 1)
                if i == NG + 1:
                    pool.wait_ge(u_ok, T)
                    pool.wait_ge(n_ok, T)
                    nc.gpsimd.iota(iota_sq, [[P, NS], [0, Q32]], base=0, channel_multiplier=0,
                                   allow_small_or_imprecise_dtypes=True).then_inc(iota_sq_ok, 1)
                for c in SPLIT[i][0]:
                    split_low(nc.gpsimd, c)
                if 1 <= i <= NG:
                    x_beta(i - 1)
                if i >= 2:
                    norm(3, i - 2)
                if i < NG:
                    norm(1, i)
                if i + 2 < NG:
                    norm(0, i + 2)
                for c in SPLIT[i][1]:
                    split_low(nc.gpsimd, c)
            for c in rest(SPLIT):
                if c not in DVE_CHUNKS:
                    split_low(nc.gpsimd, c)

            pool.wait_ge(wts_ok, 1)
            w = wts[:].rearrange("p c t -> p (c t)")
            for a in range(3):
                nc.gpsimd.tensor_tensor(wpart[:, a, :], w, zero[:, 0:Q32], ALU.add).then_inc(wpart_ok, 1)
                pool.wait_ge(wpart_ok, 2 * a + 1)
                if a < 2:
                    nc.gpsimd.tensor_tensor(wrest[:, a, :], w, wpart[:, a, :], ALU.subtract).then_inc(wpart_ok, 1)
                    pool.wait_ge(wpart_ok, 2 * a + 2)
                    w = wrest[:, a, :]
            pool.wait_ge(ohs_ok, 1)
            for a in range(2):
                nc.gpsimd.tensor_tensor(weight[:, a], ohs, bc(wpart[:, a, None, :], (P, NS, Q32)),
                                        ALU.mult).then_inc(weight_pool, 1)

            pool.wait_ge(gi_ok, 1)
            for g in range(NG):
                pool.wait_ge(flat_out[g], 16)
                pool.wait_ge(x1_out[g], 16)
            pool.wait_ge(spare_out, 16)

            def gather(s):
                if s >= NX:
                    pool.wait_ge(X_tr, s - NX + 1)
                nc.gpsimd.indirect_dma_start(X[:, s % NX, :], None, flat_dram[:, :],
                                             bass.IndirectOffsetOnAxis(gi[:, s:s + 1], 0)).then_inc(gathered[s % NX], 16)

            for s in range(NX - 1):
                gather(s)
            pool.wait_ge(route_ok, 1)
            for s in range(NS):
                if s + NX - 1 < NS:
                    gather(s + NX - 1)
                pool.wait_ge(Y_ok, s + 1)
                if s > 0:
                    pool.wait_ge(scattered, 16 * s)
                nc.gpsimd.indirect_dma_start(out[:, :], bass.IndirectOffsetOnAxis(si[:, s:s + 1], 0), Y[:, s % 2, :], None,
                                             compute_op=ALU.add).then_inc(scattered, 16)
            pool.wait_ge(scattered, 16 * NS)

        @block.scalar
        def _(act):
            def normalise(n, src, s0, dst, d0, g, done):
                act.wait_ge(nmr_ok[n], g + 1)
                for j in range(G):
                    t = G * g + j
                    nc.scalar.activation(dst[:, d0 + j, :], src[:, s0 + j, :], ACT.Identity,
                                         scale=rstd[:, n, t:t + 1], bias=nmr[:, n, t:t + 1]).then_inc(done, 1)

            def queries(g):
                act.wait_ge(x_in[g], 16)
                normalise(0, xs, G * g, qu, G * g, g, q_ok)

            def exponentials(g):
                act.wait_ge(nb_ok, g + 1)
                if g > 0:
                    act.wait_ge(pT_tr, g)
                b = g // (NG // B)
                for j in range(G):
                    t = G * g + j
                    nc.scalar.activation(prob[:, j, :], psS[:, j * B * U + b * U:j * B * U + (b + 1) * U], ACT.Exp,
                                         scale=r16[:, t:t + 1], bias=nb[:, t:t + 1],
                                         accum_out=zsum[:, t:t + 1]).then_inc(exp_ok, 1)

            def take_prob_t(g):
                act.wait_ge(pT_tr, g + 1)
                if g > 0:
                    act.wait_ge(pv_mm, 2 * g)
                nc.scalar.copy(probT[:], psPT[0:U, :]).then_inc(pT_ok, 1)

            def attention_rows(g):
                if g == 0:
                    act.wait_ge(bb3_in, 48)
                if g >= 2:
                    act.wait_ge(flat_out[g - 2], 16)
                    act.wait_ge(fT_tr, g - 1)
                normalise(1, zn, G * (g % 2), nf, G * (g % 2), g, n_ok)

            def take_n_t(g):
                act.wait_ge(nT_tr, g + 1)
                if g >= 1:
                    act.wait_ge(h_mm, KD * g)
                if g >= 2:
                    act.wait_ge(lg_mm, g - 1)
                for k in range(KD):
                    nc.scalar.copy(nT[:, k, :], psT[k][:]).then_inc(nT_ok, 1)

            def relu(g):
                if g == 0:
                    act.wait_ge(b1_ok, 1)
                else:
                    act.wait_ge(f_mm, 2 * g)
                for k in range(KD):
                    act.wait_ge(h_mm, KD * g + k + 1)
                    nc.scalar.activation(hT[:, k, :], psH[k][:], ACT.Relu, bias=b1f[:, k:k + 1]).then_inc(h_ok, 1)

            def expert_rows(g):
                act.wait_ge(nT_tr, g + 1)
                act.wait_ge(ng_ok, G * g + G)
                normalise(3, xs, G * g, nf, G * (g % 2), g, flat_ok)

            def take_f_t(g):
                act.wait_ge(fT_tr, g + 1)
                if g + 1 < NG:
                    act.wait_ge(h_mm, KD * (g + 2))
                else:
                    act.wait_ge(lg_mm, NG - 1)
                for k in range(KD):
                    nc.scalar.copy(nT[:, k, :], psT[k][:]).then_inc(fT_ok, 1)

            def split_high(c):
                act.wait_ge(stage_in[place[c]], 16 * uses(c))
                nc.scalar.copy(chunks[c][1], staged(c)).then_inc(high_ok, 1)

            act.wait_ge(kT_tr, 1)
            nc.scalar.copy(kT[:], psT[0][:, 0:B * KD * U].rearrange("p (k n) -> p k n", k=KD)).then_inc(kT_ok, 1)
            queries(0)
            exponentials(0)
            split_high(0)
            for i in range(NG + 2):
                if i < NG:
                    take_prob_t(i)
                if 1 <= i <= NG:
                    take_n_t(i - 1)
                if i + 1 < NG:
                    queries(i + 1)
                for c in ROUND[i][0]:
                    split_high(c)
                if 1 <= i <= NG:
                    relu(i - 1)
                if i >= 2:
                    expert_rows(i - 2)
                if i == NG + 1:
                    for c in ROUND_LATE:
                        split_high(c)
                if i >= 2:
                    take_f_t(i - 2)
                if i + 1 < NG:
                    exponentials(i + 1)
                if i < NG:
                    attention_rows(i)
                for c in ROUND[i][1]:
                    split_high(c)
            for c in range(max(rest(ROUND)[0], *[c + 1 for c in ROUND_LATE]), NC):
                if c == NC - 4:
                    act.wait_ge(dm_ok, 1)
                    nc.scalar.activation(ex[:], dm[:], ACT.Exp).then_inc(ex_ok, 1)
                split_high(c)

            act.wait_ge(low_dve, len(DVE_CHUNKS))
            act.wait_ge(low_pool, NC - len(DVE_CHUNKS))

            def take_xt(s, b, early=False):
                act.wait_ge(X_tr, s + 1)
                if not early:
                    act.wait_ge(val_mm, s - 1)
                ps = psX[:, 0:D].rearrange("p (k n) -> p k n", k=KD)
                nc.scalar.copy(XTh[:, b, :, :], ps).then_inc(XTh_ok, 1)
                nc.scalar.copy(XTb[:, b, :, :], ps).then_inc(XTb_ok, 1)

            def silu(s, b, early=False):
                act.wait_ge(gate_mm, s + 1)
                if not early:
                    act.wait_ge(A_ok, s - 1)
                nc.scalar.activation(S[:, b, :], psG[b][:], ACT.Silu).then_inc(silu_ok, 1)

            def take_at(s, first=False):
                act.wait_ge(A_tr, s + 1)
                if not first:
                    act.wait_ge(y_mm, s)
                ps = psA[:].rearrange("p (k n) -> p k n", k=KF)
                nc.scalar.copy(ATh[:], ps).then_inc(ATh_ok, 1)
                nc.scalar.copy(ATb[:], ps).then_inc(ATb_ok, 1)

            def weigh(s, b, early=False):
                act.wait_ge(y_mm, s + 1)
                if not early:
                    act.wait_ge(scattered, 16 * (s - 1))
                nc.scalar.activation(Y[:, b, :], psY[b][:, 0:D], ACT.Copy, scale=slotw[:, bass.ds(s, 1)]).then_inc(Y_ok, 1)

            take_xt(0, 0, True)
            silu(0, 0, True)
            take_xt(1, 1, True)
            silu(1, 1, True)
            take_at(0, True)
            take_xt(2, 0)
            act.wait_ge(slotw_ok, 1)
            weigh(0, 0, True)
            silu(2, 0)
            take_at(1)
            take_xt(3, 1)
            weigh(1, 1, True)
            with act.Fori(0, (NS - 5) // 2) as i:
                for b in (1, 0):
                    s = 2 * i + 4 - b
                    silu(s, b)
                    take_at(s - 1)
                    take_xt(s + 1, 1 - b)
                    weigh(s - 1, 1 - b)
            silu(NS - 2, 1)
            take_at(NS - 3)
            take_xt(NS - 1, 0)
            weigh(NS - 3, 0)
            silu(NS - 1, 0)
            take_at(NS - 2)
            weigh(NS - 2, 1)
            take_at(NS - 1)
            weigh(NS - 1, 0)

        @block.vector
        def _(dve):
            dve.wait_ge(kv_in, 16)
            for b in range(B):
                nc.vector.bn_stats(kst[:, b, :], kv[:, b, :]).then_inc(k_stats, 1)
            dve.wait_ge(k_stats, B)
            for b in range(B):
                nc.vector.bn_aggr(kmv[:, b, :], kst[:, b, :]).then_inc(k_mean, 1)
            dve.wait_ge(k_mean, B)
            for b in range(B):
                nc.vector.tensor_scalar(kc[:, b, :], kv[:, b, :], kmv[:, b, 0:1], None, ALU.subtract).then_inc(k_cent, 1)

            def norm_stats(n, g, src, s0):
                if g > 0:
                    dve.wait_ge(mv_ok[n], G * g)
                for j in range(G):
                    nc.vector.bn_stats(st[:, n, j, :], src[:, s0 + j, :]).then_inc(stats_d[n], 1)
                dve.wait_ge(stats_d[n], G * g + G)
                if g > 0:
                    dve.wait_ge(ve_ok[n], g)
                for j in range(G):
                    nc.vector.bn_aggr(mv[:, n, j, :], st[:, n, j, :]).then_inc(mv_ok[n], 1)

            def maxima(g):
                ts, b = slice(G * g, G * g + G), g // (NG // B)
                dve.wait_ge(score_mm, g + 1)
                sc = psS[:, :].rearrange("p (t u) -> p t u", t=G)[:, :, b * U:(b + 1) * U]
                nc.vector.reduce_max(mx[:, ts], sc, AX.X).then_inc(mx_ok, 1)
                dve.wait_ge(mx_ok, g + 1)
                dve.wait_ge(r16_ok, g + 1)
                nc.vector.scalar_tensor_tensor(out=nb[:, ts], in0=mx[:, ts], scalar=-1.0, in1=r16[:, ts],
                                               op0=ALU.mult, op1=ALU.mult).then_inc(nb_ok, 1)

            def attended(g):
                ts = slice(G * g, G * g + G)
                dve.wait_ge(exp_ok, G * g + G)
                nc.vector.reciprocal(rz[:, ts], zsum[:, ts]).then_inc(rz_ok, 1)
                dve.wait_ge(rz_ok, g + 1)
                dve.wait_ge(q_ok, G * g + G)
                if g >= 2:
                    dve.wait_ge(u_ok, G * (g - 1))
                for j in range(G):
                    t, r = G * g + j, G * (g % 2) + j
                    if j % 2 == 0:
                        dve.wait_ge(pv_mm, 2 * g + j // 2 + 1)
                    nc.vector.scalar_tensor_tensor(out=zn[:, r, :], in0=psO[j // 2][:, (j % 2) * D:(j % 2 + 1) * D],
                                                   scalar=rz[:, t:t + 1], in1=qu[:, t, :],
                                                   op0=ALU.mult, op1=ALU.add).then_inc(z_ok, 1)

            def z_stats(g):
                dve.wait_ge(z_ok, G * g + G)
                norm_stats(1, g, zn, G * (g % 2))

            def ffn_sum(g):
                for j in range(G):
                    t, r = G * g + j, G * (g % 2) + j
                    dve.wait_ge(ng_ok, t + 1)
                    if j % 2 == 0:
                        dve.wait_ge(f_mm, 2 * g + j // 2 + 1)
                    nc.vector.tensor_tensor(qu[:, t, :], psO[j // 2][:, (j % 2) * D:(j % 2 + 1) * D], zn[:, r, :],
                                            ALU.add).then_inc(u_ok, 1)
                dve.wait_ge(u_ok, G * g + G)
                norm_stats(2, g, qu, G * g)

            def after_attention(g):
                dve.wait_ge(rstd_ok[2], g + 1)
                for t in range(G * g, G * g + G):
                    nc.vector.scalar_tensor_tensor(out=qu[:, t, :], in0=qu[:, t, :], scalar=ve[:, 2, t, 0:1],
                                                   in1=gammaB[:], op0=ALU.subtract, op1=ALU.mult).then_inc(v_ok, 1)
                dve.wait_ge(v_ok, G * g + G)
                dve.wait_ge(xb_ok, G * g + G)
                for t in range(G * g, G * g + G):
                    nc.vector.scalar_tensor_tensor(out=xs[:, t, :], in0=qu[:, t, :], scalar=rstd[:, 2, t:t + 1],
                                                   in1=xs[:, t, :], op0=ALU.mult, op1=ALU.add).then_inc(x1_ok, 1)
                dve.wait_ge(x1_ok, G * g + G)
                norm_stats(3, g, xs, G * g)

            def take_logits(g):
                dve.wait_ge(lg_mm, g + 1)
                nc.vector.tensor_copy(lg[:, G * g:G * g + G, :],
                                      psH[1][:, :].rearrange("p (t n) -> p t n", t=G)[:, :, 0:E]).then_inc(lg_ok, 1)

            def x_stats(g):
                dve.wait_ge(x_in[g], 16)
                norm_stats(0, g, xs, G * g)

            x_stats(0)
            dve.wait_ge(vec_in, 48)
            nc.vector.tensor_tensor(bb[:, 0, :], rows[0:1, 0, :], rows[0:1, 1, :], ALU.add).then_inc(bb_d, 1)
            for a in range(3):
                dve.wait_ge(bb_d, 2 * a + 1)
                nc.vector.tensor_copy(bbp[:, a, :], bb[:, a, :]).then_inc(bb_ok if a == 2 else bb_d, 1)
                if a < 2:
                    dve.wait_ge(bb_d, 2 * a + 2)
                    nc.vector.tensor_tensor(bb[:, a + 1, :], bb[:, a, :], bbp[:, a, :], ALU.subtract).then_inc(bb_d, 1)
            maxima(0)
            x_stats(1)
            dve.wait_ge(aw_in, 32)
            for k in range(KD):
                nc.vector.tensor_scalar(aw1g[:, k, :], aw1[:, k, :], cols[:, 0, k:k + 1], None, ALU.mult).then_inc(w1g_ok, 1)
            dve.wait_ge(b1_mm, 1)
            nc.vector.tensor_tensor(b1f[:], psH[0][:, 0:KD], cols[:, 2, :], ALU.add).then_inc(b1_ok, 1)
            for i in range(NG + 3):
                if i >= 3:
                    take_logits(i - 3)
                if i < len(DVE_SPLIT):
                    for c in DVE_SPLIT[i][0]:
                        split_low(nc.vector, c)
                if 2 <= i <= NG + 1:
                    after_attention(i - 2)
                if i < len(DVE_SPLIT):
                    for c in DVE_SPLIT[i][1]:
                        split_low(nc.vector, c)
                if i < NG:
                    attended(i)
                    z_stats(i)
                if i + 1 < NG:
                    maxima(i + 1)
                if i + 2 < NG:
                    x_stats(i + 2)
                if 1 <= i <= NG:
                    ffn_sum(i - 1)

            n = [0]

            def link(ins):
                n[0] += 1
                ins.then_inc(step, 1)
                dve.wait_ge(step, n[0])

            v = nc.vector
            TE = (P, T, E)
            dve.wait_ge(const_ok, 2)
            dve.wait_ge(lg_ok, NG)
            dve.wait_ge(n_ok, T)
            prioB = bc(prio[:, None, :], TE)
            for c in range(TOPK):
                src = (lg, lg2)[c]
                link(v.reduce_max(m12[:, c, :], src[:], AX.X))
                link(v.tensor_tensor(pick[:], src[:], bc(m12[:, c, :, None], TE), ALU.is_ge))
                link(v.tensor_tensor(pick[:], pick[:], prioB, ALU.mult))
                link(v.reduce_max(pmax[:, c, :], pick[:], AX.X))
                link(v.tensor_tensor(oh[:, c, :, :], bc(pmax[:, c, :, None], TE), prioB, ALU.is_equal))
                if c == 0:
                    link(v.scalar_tensor_tensor(out=lg2[:], in0=oh[:, 0, :, :], scalar=-3e38, in1=lg[:],
                                                op0=ALU.mult, op1=ALU.add))
            v.tensor_tensor(dm[:], m12[:, 1, :], m12[:, 0, :], ALU.subtract).then_inc(dm_ok, 1)
            v.tensor_tensor(both[:].rearrange("p (t e) -> p t e", t=T), oh[:, 0, :, :], oh[:, 1, :, :], ALU.add).then_inc(both_ok, 1)
            dve.wait_ge(count_mm, 1)
            dve.wait_ge(ex_ok, 1)
            v.tensor_scalar(den[:], ex[:], 1.0, None, ALU.add).then_inc(step, 1)
            n[0] += 1
            link(v.tensor_copy(totE[:], psC[:, T * E:2 * T * E].rearrange("p (t e) -> p e t", t=T)))
            v.reciprocal(wts[:, 0, :], den[:]).then_inc(step, 1)
            n[0] += 1
            link(v.tensor_tensor_scan(incl[:].rearrange("p e t -> p (e t)"), first0[:].rearrange("p e t -> p (e t)"),
                                      totE[:].rearrange("p e t -> p (e t)"), 0.0, ALU.mult, ALU.add))
            v.tensor_tensor(wts[:, 1, :], ex[:], wts[:, 0, :], ALU.mult).then_inc(wts_ok, 1)
            v.tensor_scalar(tp[:], incl[:, :, T - 1], float(P - 1), None, ALU.add).then_inc(step, 1)
            n[0] += 1
            link(v.tensor_tensor(excl[:], incl[:], totE[:], ALU.subtract))
            link(v.tensor_scalar(nti[:], tp[:], ROUND_DOWN, None, ALU.bitwise_and))
            link(v.tensor_copy(ntf[:], nti[:]))
            link(v.tensor_tensor_scan(ends[:], ones8[:], ntf[:], 0.0, ALU.mult, ALU.add))
            link(v.tensor_tensor(starts[:], ends[:], ntf[:], ALU.subtract))
            link(v.tensor_tensor(base[:], bc(starts[:, None, :], TE), excl[:].rearrange("p e t -> p t e"), ALU.add))
            link(v.tensor_tensor(rank[:], psC[:, 0:T * E].rearrange("p (t e) -> p t e", t=T), base[:], ALU.add))
            link(v.tensor_tensor(rsel[:], oh[:], bc(rank[:, None, :, :], (P, TOPK, T, E)), ALU.mult))
            link(v.reduce_sum(pos[:].rearrange("p (c t) -> p c t", c=TOPK), rsel[:], AX.X))
            link(v.tensor_copy(posi[:], pos[:]))
            v.tensor_scalar(hii[:], posi[:], ROUND_DOWN, None, ALU.bitwise_and).then_inc(step, 1)
            n[0] += 1
            link(v.tensor_scalar(loi[:], posi[:], P - 1, None, ALU.bitwise_and))
            v.tensor_copy(hib[:], hii[:]).then_inc(step, 1)
            n[0] += 1
            link(v.tensor_copy(lof[:], loi[:]))
            dve.wait_ge(flat_out[NG - 2], 16)
            dve.wait_ge(flat_out[NG - 1], 16)
            dve.wait_ge(fT_tr, NG)
            dve.wait_ge(lg_mm, NG)
            dve.wait_ge(iota_sq_ok, 1)
            SQ = (P, NS, Q32)
            v.tensor_tensor(ohs, iota_sq, bc(hib[:, None, :], SQ), ALU.is_equal).then_inc(ohs_ok, 1)
            dve.wait_ge(ohs_ok, 1)
            v.tensor_tensor(whose[:, 0], ohs, bc(qp1[:, None, :], SQ), ALU.mult).then_inc(whose_ok, 1)
            v.tensor_scalar(whose[:, 1], ohs, pcol[:, 2:3], None, ALU.mult).then_inc(whose_ok, 1)
            for half in (1, 0):
                for c in range(NC):
                    if place[c] == 2 + half and c not in DVE_CHUNKS:
                        wait_split(dve, c)
                for q in range(half * Q32 // 2, (half + 1) * Q32 // 2):
                    v.tensor_scalar(ohlo[:, q, :], iota_p[:], lof[:, q:q + 1], None, ALU.is_equal).then_inc(ohlo_ok, 1)
            dve.wait_ge(wpart_ok, 5)
            v.tensor_tensor(weight[:, 2], ohs, bc(wpart[:, 2, None, :], SQ), ALU.mult).then_inc(weight_dve, 1)
            dve.wait_ge(slot_mm, 1)
            which, row = psR[:, 0:NS], psR[:, NS:2 * NS]
            v.tensor_scalar(sk[:], which, T + 0.5, -float(N), ALU.is_gt, ALU.mult).then_inc(step, 1)
            v.tensor_scalar(padg[:], which, 0.5, pcol[:, 0:1], ALU.is_lt, ALU.mult).then_inc(step, 1)
            v.tensor_scalar(pads[:], which, 0.5, pcol[:, 1:2], ALU.is_lt, ALU.mult).then_inc(step, 1)
            n[0] += 3
            link(v.tensor_scalar(sval[:], which, float(P), None, ALU.mult))
            link(v.tensor_tensor(sk[:], sk[:], sval[:], ALU.add))
            link(v.tensor_tensor(stok[:], sk[:], row, ALU.add))
            v.scalar_tensor_tensor(out=gi[:], in0=padg[:], scalar=-float(P), in1=stok[:], op0=ALU.add, op1=ALU.add).then_inc(gi_ok, 1)
            v.scalar_tensor_tensor(out=si[:], in0=pads[:], scalar=-float(P), in1=stok[:], op0=ALU.add, op1=ALU.add).then_inc(route_ok, 1)
            link(v.tensor_tensor(ge[:], bc(iota_s[0:1, :, None], (1, NS, E)), bc(ends[0:1, None, :], (1, NS, E)), ALU.is_ge))
            link(v.reduce_sum(eidf[:], ge[:], AX.X))
            v.tensor_scalar(eid[:], eidf[:], float(E - 1), None, ALU.min).then_inc(eid_ok, 1)
            dve.wait_ge(weight_mm, 1)
            link(v.tensor_copy(w01[:], psW[:, 0:NS]))
            link(v.tensor_tensor(w01[:], w01[:], psW[:, NS:2 * NS], ALU.add))
            v.tensor_tensor(slotw[:], w01[:], psW[:, 2 * NS:3 * NS], ALU.add).then_inc(slotw_ok, 1)

            def product(s, b, early=False):
                dve.wait_ge(val_mm, s + 1)
                dve.wait_ge(silu_ok, s + 1)
                if not early:
                    dve.wait_ge(A_tr, s - 1)
                v.tensor_tensor(A[:, b, :], psV[b][:], S[:, b, :], ALU.mult).then_inc(A_ok, 1)

            def low_xt(s, b, early=False):
                dve.wait_ge(XTh_ok, s + 1)
                dve.wait_ge(XTb_ok, s + 1)
                if not early:
                    dve.wait_ge(val_mm, s - 1)
                v.tensor_tensor(XTl[:, b, :, :], psX[:, 0:D].rearrange("p (k n) -> p k n", k=KD),
                                XTh[:, b, :, :].bitcast(f32), ALU.subtract).then_inc(XTl_ok, 1)

            def low_at(s, first=False):
                dve.wait_ge(ATh_ok, s + 1)
                dve.wait_ge(ATb_ok, s + 1)
                if not first:
                    dve.wait_ge(y_mm, s)
                v.tensor_tensor(ATl[:], psA[:].rearrange("p (k n) -> p k n", k=KF), ATh[:].bitcast(f32),
                                ALU.subtract).then_inc(ATl_ok, 1)

            low_xt(0, 0, True)
            low_xt(1, 1, True)
            product(0, 0, True)
            low_at(0, True)
            low_xt(2, 0)
            product(1, 1, True)
            low_at(1)
            low_xt(3, 1)
            product(2, 0)
            with dve.Fori(0, (NS - 5) // 2) as i:
                for b in (1, 0):
                    s = 2 * i + 4 - b
                    low_at(s - 1)
                    low_xt(s + 1, 1 - b)
                    product(s, b)
            low_at(NS - 3)
            low_xt(NS - 1, 0)
            product(NS - 2, 1)
            low_at(NS - 2)
            product(NS - 1, 0)
            low_at(NS - 1)

        @block.tensor
        def _(pe):
            pe.wait_ge(ident_ok, 1)
            pe.wait_ge(k_cent, B)
            for k in range(KD):
                for b in range(B):
                    c = (k * B + b) * U
                    last = nc.tensor.transpose(psT[0][:, c:c + U], kc[:, b, k * P:(k + 1) * P], ident[0:U, 0:U])
            last.then_inc(kT_tr, 1)

            def scores(g):
                pe.wait_ge(xT_in[g], 16)
                if g == 0:
                    pe.wait_ge(kT_ok, 1)
                else:
                    pe.wait_ge(exp_ok, G * g)
                for j in range(G):
                    for k in range(KD):
                        last = nc.tensor.matmul(psS[:, j * B * U:(j + 1) * B * U], xTs[:, g % 2, k, j * P:(j + 1) * P], kT[:, k, :],
                                                start=(k == 0), stop=(k == KD - 1))
                last.then_inc(score_mm, 1)

            def prob_t(g):
                pe.wait_ge(exp_ok, G * g + G)
                if g > 0:
                    pe.wait_ge(pT_ok, g)
                for j in range(G):
                    last = nc.tensor.transpose(psPT[0:U, j * P:(j + 1) * P], prob[:, j, :], ident[:])
                last.then_inc(pT_tr, 1)

            def pv(g):
                pe.wait_ge(pT_ok, g + 1)
                for j in range(G):
                    if j % 2 == 0:
                        if g == 1:
                            pe.wait_ge(z_ok, j + 2)
                        elif g > 1:
                            pe.wait_ge(u_ok, G * (g - 2) + j + 2)
                    last = nc.tensor.matmul(psO[j // 2][:, (j % 2) * D:(j % 2 + 1) * D], probT[:, j * P:(j + 1) * P],
                                            kv[:, g // (NG // B), :], start=True, stop=True)
                    if j % 2 == 1:
                        last.then_inc(pv_mm, 1)

            def rows_t(g, ready, tr):
                for j in range(G):
                    pe.wait_ge(ready, G * g + j + 1)
                    for k in range(KD):
                        last = nc.tensor.transpose(psT[k][:, j * P:(j + 1) * P], nf[:, G * (g % 2) + j, k * P:(k + 1) * P],
                                                   ident[:])
                last.then_inc(tr, 1)

            def attention_t(g):
                if g == 1:
                    pe.wait_ge(nT_ok, KD)
                elif g > 1:
                    pe.wait_ge(fT_ok, KD * (g - 1))
                rows_t(g, n_ok, nT_tr)

            def ffn_up(g):
                pe.wait_ge(nT_ok, KD * (g + 1))
                if g == 0:
                    pe.wait_ge(w1g_ok, KD)
                    pe.wait_ge(b1_ok, 1)
                for m in range(KD):
                    if g > 0:
                        pe.wait_ge(h_ok, KD * (g - 1) + m + 1)
                    if m == 1 and g >= 2:
                        pe.wait_ge(lg_ok, g - 1)
                    for k in range(KD):
                        last = nc.tensor.matmul(psH[m][:], aw1g[:, k, m * P:(m + 1) * P], nT[:, k, :],
                                                start=(k == 0), stop=(k == KD - 1))
                    last.then_inc(h_mm, 1)

            def ffn_down(g, half):
                pe.wait_ge(h_ok, KD * (g + 1))
                if g == 0:
                    pe.wait_ge(aw_in, 32)
                    pe.wait_ge(bb3_in, 48)
                    pe.wait_ge(ones3_ok, 1)
                for j in (2 * half, 2 * half + 1):
                    if j % 2 == 0:
                        if g + 1 < NG:
                            pe.wait_ge(z_ok, G * (g + 1) + j + 2)
                        else:
                            pe.wait_ge(u_ok, G * (g - 1) + j + 2)
                    o = psO[j // 2][:, (j % 2) * D:(j % 2 + 1) * D]
                    for k in range(KD):
                        nc.tensor.matmul(o, hT[:, k, j * P:(j + 1) * P], aw2[:, k, :], start=(k == 0), stop=False)
                    last = nc.tensor.matmul(o, ones3[:], bb3[:], start=False, stop=True)
                    if j % 2 == 1:
                        last.then_inc(f_mm, 1)

            def expert_t(g):
                if g + 1 < NG:
                    pe.wait_ge(nT_ok, KD * (g + 2))
                else:
                    pe.wait_ge(fT_ok, KD * (NG - 1))
                rows_t(g, flat_ok, fT_tr)

            def logits(g):
                pe.wait_ge(fT_ok, KD * (g + 1))
                if g == 0:
                    pe.wait_ge(wr_in, 16)
                if g + 1 < NG:
                    pe.wait_ge(h_ok, KD * (g + 2))
                else:
                    pe.wait_ge(lg_ok, NG - 1)
                for j in range(G):
                    for k in range(KD):
                        last = nc.tensor.matmul(psH[1][:, j * P:(j + 1) * P], nT[:, k, j * P:(j + 1) * P], wr[:, k, :],
                                                start=(k == 0), stop=(k == KD - 1))
                last.then_inc(lg_mm, 1)

            scores(0)
            pe.wait_ge(aw_in, 32)
            pe.wait_ge(vec_in, 48)
            for m in range(KD):
                for k in range(KD):
                    last = nc.tensor.matmul(psH[0][:, m:m + 1], aw1[:, k, m * P:(m + 1) * P], cols[:, 1, k:k + 1],
                                            start=(k == 0), stop=(k == KD - 1))
            last.then_inc(b1_mm, 1)
            for i in range(NG + 2):
                if i < NG:
                    prob_t(i)
                if 1 <= i <= NG:
                    attention_t(i - 1)
                if i < NG:
                    pv(i)
                if 1 <= i <= NG:
                    ffn_up(i - 1)
                if i + 1 < NG:
                    scores(i + 1)
                if 1 <= i <= NG:
                    ffn_down(i - 1, 0)
                if i == NG:
                    ffn_down(i - 1, 1)
                if i >= 2:
                    expert_t(i - 2)
                if 1 <= i < NG:
                    ffn_down(i - 1, 1)
                if i >= 2:
                    logits(i - 2)

            pe.wait_ge(both_ok, 1)
            nc.tensor.matmul(psC[:, 0:T * E], tri[:], both[:], start=True, stop=True)
            nc.tensor.matmul(psC[:, T * E:2 * T * E], onesb[:], both[:], start=True, stop=True).then_inc(count_mm, 1)
            pe.wait_ge(whose_ok, 2)
            for i in range(Q32):
                q = (i + Q32 // 2) % Q32
                pe.wait_ge(ohlo_ok, i + 1)
                last = nc.tensor.matmul(psR[:, 0:2 * NS], ohlo[:, q, :], whose[:, :, :, q].rearrange("p a s -> p (a s)"),
                                        start=(i == 0), stop=(i == Q32 - 1))
            last.then_inc(slot_mm, 1)

            pe.wait_ge(weight_pool, 2)
            pe.wait_ge(weight_dve, 1)
            for q in range(Q32):
                last = nc.tensor.matmul(psW[:, 0:3 * NS], ohlo[:, q, :], weight[:, :, :, q].rearrange("p a s -> p (a s)"),
                                        start=(q == 0), stop=(q == Q32 - 1))
            last.then_inc(weight_mm, 1)

            pe.wait_ge(eid_ok, 1)
            pe.wait_ge(high_ok, NC)
            pe.wait_ge(low_dve, len(DVE_CHUNKS))
            pe.wait_ge(low_pool, NC - len(DVE_CHUNKS))

            expert_regs = [pe.alloc_register(f"expert{j}") for j in range(NX)]

            def load_expert(s, j):
                pe.reg_load(expert_regs[j % NX], eid[0:1, bass.ds(s, 1)])

            def expert(j):
                return pe.snap(expert_regs[j % NX], min_val=0, max_val=E - 1)

            def w1_at(w, e, k, h):
                return w[:, bass.ds(e, 1), k, h * F:(h + 1) * F].rearrange("p a f -> p (a f)")

            def w2_at(w, e, k):
                return w[:, bass.ds(e, 1), k, :].rearrange("p a c -> p (a c)")

            def rows_in(s, x, n, first=False):
                pe.wait_ge(gathered[x], 16 * n)
                if not first:
                    pe.wait_ge(XTl_ok, s)
                for k in range(KD):
                    last = nc.tensor.transpose(psX[:, k * P:(k + 1) * P], X[:, x, k * P:(k + 1) * P], ident[:])
                last.then_inc(X_tr, 1)

            def gate(s, b, e, early=False):
                pe.wait_ge(XTh_ok, s + 1)
                if not early:
                    pe.wait_ge(silu_ok, s - 1)
                for k in range(KD):
                    nc.tensor.matmul(psG[b][:], XTh[:, b, k, :], w1_at(W1h, e, k, 1), start=(k == 0), stop=False)
                pe.wait_ge(XTb_ok, s + 1)
                for k in range(KD):
                    nc.tensor.matmul(psG[b][:], XTb[:, b, k, :], w1_at(W1l, e, k, 1), start=False, stop=False)
                pe.wait_ge(XTl_ok, s + 1)
                for k in range(KD):
                    last = nc.tensor.matmul(psG[b][:], XTl[:, b, k, :], w1_at(W1h, e, k, 1), start=False, stop=(k == KD - 1))
                last.then_inc(gate_mm, 1)

            def val(s, b, e, early=False):
                if not early:
                    pe.wait_ge(A_ok, s - 1)
                parts = ((XTh, W1h), (XTb, W1l), (XTl, W1h))
                for i, (xp, wp) in enumerate(parts):
                    for k in range(KD):
                        last = nc.tensor.matmul(psV[b][:], xp[:, b, k, :], w1_at(wp, e, k, 0),
                                                start=(i == 0 and k == 0), stop=(i == 2 and k == KD - 1))
                last.then_inc(val_mm, 1)

            def act_t(s, b, first=False):
                pe.wait_ge(A_ok, s + 1)
                if not first:
                    pe.wait_ge(ATl_ok, s)
                for k in range(KF):
                    last = nc.tensor.transpose(psA[:, k * P:(k + 1) * P], A[:, b, k * P:(k + 1) * P], ident[:])
                last.then_inc(A_tr, 1)

            def down(s, b, e, early=False):
                pe.wait_ge(ATh_ok, s + 1)
                if not early:
                    pe.wait_ge(Y_ok, s - 1)
                for k in range(KF):
                    nc.tensor.matmul(psY[b][:, 0:D], ATh[:, k, :], w2_at(W2h, e, k), start=(k == 0), stop=False)
                pe.wait_ge(ATb_ok, s + 1)
                for k in range(KF):
                    nc.tensor.matmul(psY[b][:, 0:D], ATb[:, k, :], w2_at(W2l, e, k), start=False, stop=False)
                pe.wait_ge(ATl_ok, s + 1)
                for k in range(KF):
                    last = nc.tensor.matmul(psY[b][:, 0:D], ATl[:, k, :], w2_at(W2h, e, k), start=False, stop=(k == KF - 1))
                last.then_inc(y_mm, 1)

            def steady(s, j, n, last=False):
                b, e = j % 2, expert(j)
                if not last:
                    load_expert(s + 1, j + 1)
                down(s - 2, b, expert(j - 2))
                gate(s, b, e)
                act_t(s - 1, 1 - b)
                val(s, b, e)
                if not last:
                    rows_in(s + 1, (j + 1) % NX, n)

            for s in range(3):
                load_expert(s, s)
            rows_in(0, 0, 1, True)
            gate(0, 0, expert(0), True)
            val(0, 0, expert(0), True)
            rows_in(1, 1, 1)
            gate(1, 1, expert(1), True)
            act_t(0, 0, True)
            val(1, 1, expert(1), True)
            rows_in(2, 2, 1)
            load_expert(3, 3)
            down(0, 0, expert(0), True)
            gate(2, 0, expert(2))
            act_t(1, 1)
            val(2, 0, expert(2))
            rows_in(3, 3, 1)
            pe.wait_ge(slotw_ok, 1)
            rounds = (NS - 3) // NX
            with pe.Fori(0, rounds - 1) as i:
                for j in range(NX):
                    steady(NX * i + 3 + j, 3 + j, i + 2)
            for j in range(NX):
                steady(NX * (rounds - 1) + 3 + j, 3 + j, rounds + 1, j == NX - 1)
            down(NS - 2, 1, expert(NS - 2))
            act_t(NS - 1, 0)
            down(NS - 1, 0, expert(NS - 1))


def kernel(x, ctx_1024, L0_xattn_W1, L0_xattn_b1, L0_xattn_W2, L0_xattn_b2, L0_xattn_gamma, L0_xattn_beta,
           L0_ffn_Wr, L0_ffn_W1, L0_ffn_W2):
    import numpy as np
    import concourse.bacc as bacc
    from concourse import mybir
    from concourse.bass_utils import run_bass_kernel_spmd

    x = np.asarray(x)
    Bb, R, D = x.shape
    N = Bb * R
    flat = np.ascontiguousarray(x.reshape(N, D))
    ins = {
        "x": flat,
        "xT": np.ascontiguousarray(flat.T),
        "ctx_kv": np.ascontiguousarray(ctx_1024),
        "aW1": np.ascontiguousarray(L0_xattn_W1),
        "aW2": np.ascontiguousarray(L0_xattn_W2),
        "vec_cols": np.ascontiguousarray(np.stack([L0_xattn_gamma, L0_xattn_beta, L0_xattn_b1])
                                         .reshape(3, D // 128, 128).transpose(2, 0, 1)),
        "b2": np.ascontiguousarray(L0_xattn_b2),
        "gamma": np.ascontiguousarray(L0_xattn_gamma),
        "beta": np.ascontiguousarray(L0_xattn_beta),
        "WrT": np.ascontiguousarray(np.asarray(L0_ffn_Wr).T),
        "eW1": np.ascontiguousarray(np.asarray(L0_ffn_W1).transpose(0, 2, 1)),
        "eW2": np.ascontiguousarray(np.asarray(L0_ffn_W2).transpose(0, 2, 1)),
    }
    nc = bacc.Bacc("TRN2", target_bir_lowering=False, num_devices=1)
    aps = [nc.dram_tensor(f"in_{k}", v.shape, mybir.dt.from_np(v.dtype), kind="ExternalInput").ap() for k, v in ins.items()]
    flat_dram = nc.dram_tensor("flat_rows", (N, D), mybir.dt.float32, kind="Internal").ap()
    out = nc.dram_tensor("out_rows", (N + 128, D), mybir.dt.float32, kind="ExternalOutput").ap()
    xattn_then_sparse_experts(nc, *aps, flat_dram, out)
    r = run_bass_kernel_spmd(nc, [{f"in_{k}": v for k, v in ins.items()}], core_ids=[0])
    return r.results[0]["out_rows"][:N].reshape(Bb, R, D)
```
